# Optimizing a Trainium2 kernel written in Bass

```python
import numpy as np
import jax
import jax.numpy as jnp

def _softmax(x, axis=-1):
    return jax.nn.softmax(x, axis=axis)

def _gelu(x):
    return jax.nn.gelu(x, approximate=True)

def _silu(x):
    return jax.nn.silu(x)

def _sigmoid(x):
    return jax.nn.sigmoid(x)

def _layernorm(x, axis=-1, eps=1e-05):
    m = jnp.mean(x, axis=axis, keepdims=True)
    v = jnp.var(x, axis=axis, keepdims=True)
    return (x - m) / jnp.sqrt(v + eps)

def _scatter_add(tgt, idx, src, axis=0):
    return tgt.at[idx].add(src)

def _segment_sum(src, seg, n):
    return jax.ops.segment_sum(src, seg, n)
kernel_name = 'mk_audio_tower_d1_tok_audfeat4096_r4_644864'

def setup_inputs(seed: int=0):
    np.random.seed(seed)
    _w = jnp.asarray

    def _rec_inputs():
        import jax
        import jax.numpy as jnp
        _rk = jax.random.key(seed)
        x = 7.22013e-05 + 1.00017 * jax.random.normal(jax.random.fold_in(_rk, 1), (16, 64, 2048), jnp.float32)
        return x
    x = _rec_inputs()

    def _L0_tok_setup():
        import jax, jax.numpy as jnp
        import numpy as np
        EPS = 1e-05

        def conv1d(x, w, stride=1, pad=0, groups=1):
            return jax.lax.conv_general_dilated(x, w, window_strides=(stride,), padding=[(pad, pad)], dimension_numbers=('NCH', 'OIH', 'NCH'), feature_group_count=groups)

        def groupnorm1(x, gamma, beta):
            m = jnp.mean(x, axis=(1, 2), keepdims=True)
            v = jnp.mean((x - m) ** 2, axis=(1, 2), keepdims=True)
            xn = (x - m) * jax.lax.rsqrt(v + EPS)
            return xn * gamma[None, :, None] + beta[None, :, None]
        key = jax.random.key(seed)
        ks = jax.random.split(key, 8)
        B, C_IN, T, H = (16, 64, 2048, 128)
        x = jax.random.normal(ks[0], (B, C_IN, T), dtype=jnp.float32)
        conv_in_w = jax.random.normal(ks[1], (H, C_IN, 7), dtype=jnp.float32) * 0.05
        dw_w = jax.random.normal(ks[2], (H, 1, 5), dtype=jnp.float32) * 0.1
        dw_b = jax.random.normal(ks[3], (H,), dtype=jnp.float32) * 0.01
        pw_w = jax.random.normal(ks[4], (H, H, 1), dtype=jnp.float32) * 0.04
        gn1_w = jnp.ones((H,), jnp.float32)
        gn1_b = jnp.zeros((H,), jnp.float32)
        gn2_w = jnp.ones((H,), jnp.float32)
        gn2_b = jnp.zeros((H,), jnp.float32)
        return {'x': x, 'conv_in_w': conv_in_w, 'dw_w': dw_w, 'dw_b': dw_b, 'pw_w': pw_w, 'gn1_w': gn1_w, 'gn1_b': gn1_b, 'gn2_w': gn2_w, 'gn2_b': gn2_b}
    _L0_tok_all = _L0_tok_setup()
    _L0_tok_in = {k: v for k, v in _L0_tok_all.items() if k in ('conv_in_w', 'dw_w', 'dw_b', 'pw_w', 'gn1_w', 'gn1_b', 'gn2_w', 'gn2_b')}
    del _L0_tok_all

    def _L0_attn_setup():
        import jax, jax.numpy as jnp
        import numpy as np
        H = 1024
        NH = 32
        QR = 384
        KVR = 128
        RD = 64
        ND = 128
        VD = 128
        QK = RD + ND
        EPS = 1e-06
        THETA = 10000.0
        B, S = (2, 256)

        def rmsnorm(x, w):
            norm = jnp.sqrt(jnp.sum(x * x, axis=-1, keepdims=True)) * x.shape[-1] ** (-0.5)
            return x / (norm + EPS) * w

        def rope_cos_sin(seq_len):
            inv_freq = 1.0 / THETA ** (jnp.arange(0, RD, 2, dtype=jnp.float32) / RD)
            t = jnp.arange(seq_len, dtype=jnp.float32)
            freqs = jnp.outer(t, inv_freq)
            emb = jnp.concatenate([freqs, freqs], -1)
            return (jnp.cos(emb), jnpp_cos_sin_dummy() if False else jnp.sin(emb))

        def rotate_half(x):
            x1, x2 = jnp.split(x, 2, axis=-1)
            return jnp.concatenate([-x2, x1], axis=-1)
        key = jax.random.key(seed)
        ks = jax.random.split(key, 8)
        sc = 0.02
        return {'hidden_states': jax.random.normal(ks[0], (B, S, H), jnp.float32), 'w_qa': jax.random.normal(ks[1], (H, QR), jnp.float32) * sc, 'g_qa': jnp.ones((QR,), jnp.float32), 'w_qb': jax.random.normal(ks[2], (QR, NH * QK), jnp.float32) * sc, 'w_kva': jax.random.normal(ks[3], (H, KVR + RD), jnp.float32) * sc, 'g_kva': jnp.ones((KVR,), jnp.float32), 'w_kvb': jax.random.normal(ks[4], (KVR, NH * (ND + VD)), jnp.float32) * sc, 'w_o': jax.random.normal(ks[5], (NH * VD, H), jnp.float32) * sc}
    _L0_attn_all = _L0_attn_setup()
    _L0_attn_in = {k: v for k, v in _L0_attn_all.items() if k in ('w_qa', 'g_qa', 'w_qb', 'w_kva', 'g_kva', 'w_kvb', 'w_o')}
    del _L0_attn_all

    def _L0_ffn_setup():
        import jax, jax.numpy as jnp
        import numpy as np
        R = 16
        NUM_EXPERTS = 8
        TOP_K = 2
        LORA_ALPHA = 32
        SCALING = LORA_ALPHA / R
        key = jax.random.key(seed)
        ks = jax.random.split(key, 6)
        d_in, d_out = (1024, 1024)
        x = jax.random.normal(ks[0], (4, 512, d_in), dtype=jnp.float32)
        W_base = jax.random.normal(ks[1], (d_out, d_in), dtype=jnp.float32) * 0.02
        b_base = jax.random.normal(ks[2], (d_out,), dtype=jnp.float32) * 0.02
        W_router = jax.random.normal(ks[3], (NUM_EXPERTS, d_in), dtype=jnp.float32) * 0.01
        A = jax.random.normal(ks[4], (NUM_EXPERTS, R, d_in), dtype=jnp.float32) * 0.02
        B = jax.random.normal(ks[5], (NUM_EXPERTS, d_out, R), dtype=jnp.float32) * 0.02
        return {'x': x, 'W_base': W_base, 'b_base': b_base, 'W_router': W_router, 'A': A, 'B': B}
    _L0_ffn_all = _L0_ffn_setup()
    _L0_ffn_in = {k: v for k, v in _L0_ffn_all.items() if k in ('W_base', 'b_base', 'W_router', 'A', 'B')}
    del _L0_ffn_all
    return {'x': x, 'L0_tok_conv_in_w': _L0_tok_in['conv_in_w'], 'L0_tok_dw_w': _L0_tok_in['dw_w'], 'L0_tok_dw_b': _L0_tok_in['dw_b'], 'L0_tok_pw_w': _L0_tok_in['pw_w'], 'L0_tok_gn1_w': _L0_tok_in['gn1_w'], 'L0_tok_gn1_b': _L0_tok_in['gn1_b'], 'L0_tok_gn2_w': _L0_tok_in['gn2_w'], 'L0_tok_gn2_b': _L0_tok_in['gn2_b'], 'L0_attn_w_qa': _L0_attn_in['w_qa'], 'L0_attn_g_qa': _L0_attn_in['g_qa'], 'L0_attn_w_qb': _L0_attn_in['w_qb'], 'L0_attn_w_kva': _L0_attn_in['w_kva'], 'L0_attn_g_kva': _L0_attn_in['g_kva'], 'L0_attn_w_kvb': _L0_attn_in['w_kvb'], 'L0_attn_w_o': _L0_attn_in['w_o'], 'L0_ffn_W_base': _L0_ffn_in['W_base'], 'L0_ffn_b_base': _L0_ffn_in['b_base'], 'L0_ffn_W_router': _L0_ffn_in['W_router'], 'L0_ffn_A': _L0_ffn_in['A'], 'L0_ffn_B': _L0_ffn_in['B']}

def reference(x, L0_tok_conv_in_w, L0_tok_dw_w, L0_tok_dw_b, L0_tok_pw_w, L0_tok_gn1_w, L0_tok_gn1_b, L0_tok_gn2_w, L0_tok_gn2_b, L0_attn_w_qa, L0_attn_g_qa, L0_attn_w_qb, L0_attn_w_kva, L0_attn_g_kva, L0_attn_w_kvb, L0_attn_w_o, L0_ffn_W_base, L0_ffn_b_base, L0_ffn_W_router, L0_ffn_A, L0_ffn_B):
    import jax
    import jax.numpy as jnp

    def _L0_tok_ref(x, conv_in_w, dw_w, dw_b, pw_w, gn1_w, gn1_b, gn2_w, gn2_b):
        import jax, jax.numpy as jnp
        import numpy as np
        EPS = 1e-05

        def conv1d(x, w, stride=1, pad=0, groups=1):
            return jax.lax.conv_general_dilated(x, w, window_strides=(stride,), padding=[(pad, pad)], dimension_numbers=('NCH', 'OIH', 'NCH'), feature_group_count=groups)

        def groupnorm1(x, gamma, beta):
            m = jnp.mean(x, axis=(1, 2), keepdims=True)
            v = jnp.mean((x - m) ** 2, axis=(1, 2), keepdims=True)
            xn = (x - m) * jax.lax.rsqrt(v + EPS)
            return xn * gamma[None, :, None] + beta[None, :, None]
        H = conv_in_w.shape[0]
        h = conv1d(x, conv_in_w, stride=1, pad=3)
        h = jax.nn.gelu(groupnorm1(h, gn1_w, gn1_b), approximate=False)
        h = conv1d(h, dw_w, stride=2, pad=2, groups=H) + dw_b[None, :, None]
        h = conv1d(h, pw_w)
        h = jax.nn.gelu(groupnorm1(h, gn2_w, gn2_b), approximate=False)
        return h

    def _L0_attn_ref(hidden_states, w_qa, g_qa, w_qb, w_kva, g_kva, w_kvb, w_o):
        import jax, jax.numpy as jnp
        import numpy as np
        H = 1024
        NH = 32
        QR = 384
        KVR = 128
        RD = 64
        ND = 128
        VD = 128
        QK = RD + ND
        EPS = 1e-06
        THETA = 10000.0
        B, S = (2, 256)

        def rmsnorm(x, w):
            norm = jnp.sqrt(jnp.sum(x * x, axis=-1, keepdims=True)) * x.shape[-1] ** (-0.5)
            return x / (norm + EPS) * w

        def rope_cos_sin(seq_len):
            inv_freq = 1.0 / THETA ** (jnp.arange(0, RD, 2, dtype=jnp.float32) / RD)
            t = jnp.arange(seq_len, dtype=jnp.float32)
            freqs = jnp.outer(t, inv_freq)
            emb = jnp.concatenate([freqs, freqs], -1)
            return (jnp.cos(emb), jnpp_cos_sin_dummy() if False else jnp.sin(emb))

        def rotate_half(x):
            x1, x2 = jnp.split(x, 2, axis=-1)
            return jnp.concatenate([-x2, x1], axis=-1)
        b, s, _ = hidden_states.shape
        q_c = rmsnorm(hidden_states @ w_qa, g_qa)
        q = (q_c @ w_qb).reshape(b, s, NH, QK).transpose(0, 2, 1, 3)
        q_nope, q_rope = (q[..., :ND], q[..., ND:])
        kv = hidden_states @ w_kva
        k_c, k_rope = (kv[..., :KVR], kv[..., KVR:])
        k_c = rmsnorm(k_c, g_kva)
        kst = (k_c @ w_kvb).reshape(b, s, NH, ND + VD).transpose(0, 2, 1, 3)
        k_nope, v = (kst[..., :ND], kst[..., ND:])
        inv_freq = 1.0 / THETA ** (jnp.arange(0, RD, 2, dtype=jnp.float32) / RD)
        freqs = jnp.outer(jnp.arange(s, dtype=jnp.float32), inv_freq)
        emb = jnp.concatenate([freqs, freqs], -1)
        cos = jnp.cos(emb)[None, None]
        sin = jnp.sin(emb)[None, None]
        k_rope = k_rope[:, None]
        q_rope = q_rope * cos + rotate_half(q_rope) * sin
        k_rope = k_rope * cos + rotate_half(k_rope) * sin
        k_rope = jnp.broadcast_to(k_rope, (b, NH, s, RD))
        query = jnp.concatenate([q_nope, q_rope], -1)
        key_s = jnp.concatenate([k_nope, k_rope], -1)
        scaling = QK ** (-0.5)
        scores = jnp.einsum('bhqd,bhkd->bhqk', query, key_s) * scaling
        attn = jax.nn.softmax(scores, axis=-1)
        out = jnp.einsum('bhqk,bhkd->bhqd', attn, v)
        out = out.transpose(0, 2, 1, 3).reshape(b, s, NH * VD)
        return out @ w_o

    def _L0_ffn_ref(x, W_base, b_base, W_router, A, B):
        import jax, jax.numpy as jnp
        import numpy as np
        R = 16
        NUM_EXPERTS = 8
        TOP_K = 2
        LORA_ALPHA = 32
        SCALING = LORA_ALPHA / R
        orig_shape = x.shape
        d_in = x.shape[-1]
        x_flat = x.reshape(-1, d_in)
        logits = x_flat @ W_router.T
        probs = jax.nn.softmax(logits, axis=-1)
        topk_probs, topk_idx = jax.lax.top_k(probs, TOP_K)
        topk_probs = topk_probs / jnp.sum(topk_probs, axis=-1, keepdims=True)
        onehot = jax.nn.one_hot(topk_idx, NUM_EXPERTS, dtype=x.dtype)
        combine = jnp.einsum('nk,nke->ne', topk_probs, onehot)
        h = jnp.einsum('nd,erd->ner', x_flat, A)
        hw = h * combine[:, :, None]
        expert_out = jnp.einsum('ner,eor->no', hw, B) * SCALING
        base_out = x_flat @ W_base.T + b_base
        out = base_out + expert_out
        return out.reshape(*orig_shape[:-1], W_base.shape[0])
    h = _L0_tok_ref(x, L0_tok_conv_in_w, L0_tok_dw_w, L0_tok_dw_b, L0_tok_pw_w, L0_tok_gn1_w, L0_tok_gn1_b, L0_tok_gn2_w, L0_tok_gn2_b)
    h = h + _L0_attn_ref(_layernorm(h, axis=-1), L0_attn_w_qa, L0_attn_g_qa, L0_attn_w_qb, L0_attn_w_kva, L0_attn_g_kva, L0_attn_w_kvb, L0_attn_w_o)
    h = h + _L0_ffn_ref(_layernorm(h, axis=-1), L0_ffn_W_base, L0_ffn_b_base, L0_ffn_W_router, L0_ffn_A, L0_ffn_B)
    return h

_drawn_inputs = setup_inputs


def setup_inputs(seed=0):
    import zlib

    import numpy as np

    out = dict(_drawn_inputs(seed))
    spreads = {'L0_tok_gn1_w': (1.0, 0.2),
     'L0_tok_gn1_b': (0.0, 0.1),
     'L0_tok_gn2_w': (1.0, 0.2),
     'L0_tok_gn2_b': (0.0, 0.1),
     'L0_attn_g_qa': (1.0, 0.6),
     'L0_attn_g_kva': (1.0, 0.6)}
    factors = {'L0_attn_w_qa': 3.985, 'L0_attn_w_qb': 4.037, 'L0_ffn_b_base': 2.667}
    for name, (base, spread) in spreads.items():
        noise = np.random.default_rng([zlib.crc32(name.encode()), seed]).standard_normal(out[name].shape)
        drawn = base * np.exp(spread * noise) if base else spread * noise
        out[name] = jnp.asarray(drawn.astype(out[name].dtype))
    for name, factor in factors.items():
        out[name] = (out[name] * factor).astype(out[name].dtype)
    return out
```

```python
from contextlib import ExitStack

import concourse.bass as bass
from concourse import mybir

F32 = mybir.dt.float32
F16 = mybir.dt.float16
I32 = mybir.dt.int32
ALU = mybir.AluOpType
ACT = mybir.ActivationFunctionType
AX = mybir.AxisListType

B, CI, T, CH = 16, 64, 2048, 128
TAPS, PAD, DW_TAPS, DW_PAD = 7, 3, 5, 2
PAIRS = (TAPS + 1) // 2
D = T // 2
P = 128
KT = D // P
QR, KVR, RD, NH = 384, 128, 64, 32
QT = QR // P
QK = RD + 128
TOK = B * CH
CHUNK = 512
HEADS = 4
GROUPS = NH // HEADS
QUAD = 4
QUADS = B // QUAD
ROUNDS = GROUPS * QUADS
RAW_Q, RAW_K, RAW_V, RAW_O, RAW_R = 0, QR, QR + P, QR + 2 * P, QR + 2 * P + D
RAW = RAW_R + QT * RD
NE, RANK = 8, 16
HA = NE * RANK + NE
GN_EPS, LN_EPS, RMS_EPS = 1e-5, 1e-5, 1e-6
LORA_SCALE = 2.0
RSQRT_MAGIC = float(0x5F3759DF)
SENTINEL = -3.0e38

CW_S = 2.0**12
DW_S, PW_S = 2.0**5, 2.0**7
LN_S, AW_S = 2.0**8, 2.0**8
QC_S, KC_S = 2.0**6, 2.0**6
KR_S, QRO_S = 2.0**7, 2.0**7
WP_S, WR_S, M_S = 2.0**9, 2.0**8, 2.0**10
QP_S = QC_S * WP_S / 2.0**7
PR_S = 2.0**12
O_S = 2.0**8
HW_S, LB_S = 2.0**8, 2.0**8
GN_SCALE = CW_S
assert GN_SCALE == DW_S * PW_S
assert QP_S * KC_S == KR_S * QRO_S
assert HW_S * LB_S == LN_S * AW_S


def pipeline(eng, body, first, lags, steady, unroll=2):
    assert steady >= max(lags)
    lo, hi = steady, B + min(lags)
    hi -= (hi - lo) % unroll
    for i in range(first, lo):
        body(i, i % 2, lambda lag, i=i: 0 <= i - lag < B)
    with eng.Fori(lo, hi - unroll + 1, unroll) as r:
        for u in range(unroll):
            body(r + u if u else r, (lo + u) % 2, lambda lag: True)
    for i in range(hi, B + max(lags)):
        body(i, i % 2, lambda lag, i=i: 0 <= i - lag < B)


def newton_rsqrt(pool, link, y, v, t):
    link(pool.tensor_scalar(y.bitcast(I32), v.bitcast(I32), -0.5, RSQRT_MAGIC, ALU.mult, ALU.add))
    for _ in range(3):
        link(pool.tensor_tensor(t, y, y, ALU.mult))
        link(pool.tensor_tensor(t, t, v, ALU.mult))
        link(pool.tensor_scalar(t, t, -0.5, 1.5, ALU.mult, ALU.add))
        link(pool.tensor_tensor(y, y, t, ALU.mult))


RSQRT_LINKS = 13


def wait_apart(eng, passed, *waits):
    for sem, value in waits:
        eng.wait_ge(sem, value)
    eng.sem_inc(passed, 1)


class Chain:

    def __init__(self, eng, sem, batch, per, passed=None):
        self.eng, self.sem, self.base, self.per, self.n = eng, sem, batch * per, per, 0
        self.passed = passed

    def __call__(self, ins, apart=True):
        self.n += 1
        assert self.n <= self.per
        ins.then_inc(self.sem, 1)
        if self.n < self.per and apart:
            if self.passed:
                wait_apart(self.eng, self.passed, (self.sem, self.base + self.n))
            else:
                self.eng.wait_ge(self.sem, self.base + self.n)


def weights_stage(nc, keep, wc_d, wqk_d, pw_d, rows_d, params_d, consts_d):
    with ExitStack() as ctx:
        raw_c = ctx.enter_context(nc.sbuf_tensor("raw_c", [P, PAIRS * CH], F32))
        raw_qk = ctx.enter_context(nc.sbuf_tensor("raw_qk", [P, KT * (QR + KVR + RD)], F32))
        raw_pw = ctx.enter_context(nc.sbuf_tensor("raw_pw", [P, CH], F32))
        loaded = [ctx.enter_context(nc.semaphore(f"w_loaded{i}")) for i in range(6)]
        high = ctx.enter_context(nc.semaphore("w_high"))
        low = ctx.enter_context(nc.semaphore("w_low"))
        ident_done = ctx.enter_context(nc.semaphore("ident_done"))
        fills = ctx.enter_context(nc.semaphore("fills"))
        block = ctx.enter_context(nc.Block())
        splits = [
            (raw_c[:, :], keep["wc_h"][:, :], keep["wc_l"][:, :], CW_S),
            (raw_pw[:, :], keep["pw_h"][:, :], keep["pw_l"][:, :], PW_S),
            (raw_qk[:, :], keep["wqk_h"][:, :], keep["wqk_l"][:, :], AW_S),
        ]

        @block.sync
        def _(sp):
            sp.dma_start(raw_c[:, :], wc_d).then_inc(loaded[0], 16)
            sp.dma_start(raw_pw[:, :], pw_d).then_inc(loaded[1], 16)
            sp.dma_start(raw_qk[:, :], wqk_d).then_inc(loaded[2], 16)
            sp.dma_start(keep["consts"][:, :], consts_d).then_inc(loaded[3], 16)
            sp.dma_start(keep["params"][:, :], params_d).then_inc(loaded[4], 16)
            sp.dma_start(keep["gains"][:, :], rows_d.partition_broadcast(P)).then_inc(loaded[5], 16)
            sp.wait_ge(loaded[4], 16)
            sp.wait_ge(loaded[5], 16)

        @block.scalar
        def _(act):
            for n, (raw, h, _, s) in enumerate(splits):
                act.wait_ge(loaded[n], 16)
                act.activation(h, raw, ACT.Copy, scale=s).then_inc(high, 1)
            act.wait_ge(loaded[3], 16)
            act.activation(keep["ident_h"][:, :], keep["consts"][:, 0:P], ACT.Copy).then_inc(ident_done, 1)

        @block.vector
        def _(dve):
            dve.memset(keep["mean_mat"][:, :], 1.0 / P).then_inc(fills, 1)
            for n, (raw, h, l, s) in enumerate(splits):
                dve.wait_ge(high, n + 1)
                dve.scalar_tensor_tensor(out=l, in0=raw, scalar=s, in1=h, op0=ALU.mult,
                                         op1=ALU.subtract).then_inc(low, 1)
            dve.wait_ge(low, len(splits))


def token_phase(nc, keep, x_d):
    XW = T + 2 * PAD
    GELU1, DW, GELU2, HID, PROJ, NORM, TAIL = 1, 2, 3, 4, 5, 6, 7
    LAST = B - 1
    with ExitStack() as ctx:
        def sb(name, shape, dt=F32):
            return ctx.enter_context(nc.sbuf_tensor(name, shape, dt))

        def pb(name):
            return ctx.enter_context(nc.psum_tensor(name, [P, CHUNK], F32))

        def sem(name):
            return ctx.enter_context(nc.semaphore(name))

        x_f = sb("x_f", [P, XW])
        x_h = [sb(f"x_h{i}", [P, XW], F16) for i in range(2)]
        x_l = [sb(f"x_l{i}", [P, XW], F16) for i in range(2)]
        y1 = [sb(f"y1_{i}", [P, T]) for i in range(2)]
        g1 = sb("g1", [P, T + 2 * DW_PAD])
        dw = sb("dw", [P, D])
        dw_h, dw_l = sb("dw_h", [P, D], F16), sb("dw_l", [P, D], F16)
        hid = sb("hid", [P, D])
        ht_h, ht_l = sb("ht_h", [P, D], F16), sb("ht_l", [P, D], F16)
        q_n, k_n, kr_a, kr_b, kr2 = (sb("q_n", [P, QR]), sb("k_n", [P, KVR]), sb("kr_a", [P, RD]),
                                     sb("kr_b", [P, RD]), sb("kr2", [P, 2 * RD]))
        bn1, bn2, bn3 = sb("bn1", [P, 4, 6]), sb("bn2", [P, 2, 6]), sb("bn3", [P, 2, 6])
        st = sb("st", [P, 4])
        st3 = sb("st3", [P, 2])
        s = sb("s", [P, 4])
        msq = sb("msq", [P, 2])
        v, vm, y, t = (sb(n, [P, 5]) for n in ("v", "vm", "y", "t"))
        c12, c3 = sb("c12", [P, 4]), sb("c3", [P, 2])
        junk, ss, nrm, rinv = sb("junk", [P, QR]), sb("ss", [P, 2]), sb("nrm", [P, 2]), sb("rinv", [P, 2])
        conv_ps = [pb("conv_ps0"), pb("conv_ps1")]
        stat_ps, turn_ps = pb("stat_ps"), pb("turn_ps")
        pw_ps = [pb("pw_ps0"), pb("pw_ps1")]
        q_ps, kv_ps = pb("q_ps"), pb("kv_ps")
        (pool_passed, dve_passed, zeroed, zeroed_x, x_loaded, x_hi, x_lo, conv_done, y1_copied, bn1_done,
         st1_ready, st2_ready, stat_done, s_copied, norm_step, gelu1_done, dw_step, dw_hi, dw_lo, pw_done,
         bn2_done, gelu2_done, ln_step, hid_done, ht_done, ht_hi, ht_lo, proj_done, ss_done, rinv_done,
         qn_done, kn_done, kr_step, tail1_done, tail2_done, t1_hi, t1_lo, kc_hi, kc_lo, t2_hi,
         t2_lo) = (sem(n) for n in (
             "pool_passed dve_passed zeroed zeroed_x x_loaded x_hi x_lo conv_done y1_copied bn1_done "
             "st1_ready st2_ready stat_done s_copied norm_step gelu1_done dw_step dw_hi dw_lo pw_done "
             "bn2_done gelu2_done ln_step hid_done ht_done ht_hi ht_lo proj_done ss_done rinv_done "
             "qn_done kn_done kr_step tail1_done tail2_done t1_hi t1_lo kc_hi kc_lo t2_hi t2_lo").split())
        GN_STEPS, LN_STEPS, NORM_STEPS = 23, 25, 28
        params, gains, resid = keep["params"], keep["gains"], keep["resid"]
        ident = keep["consts"][:, 0:P]
        cos, sin = keep["consts"][:, P:P + RD], keep["consts"][:, P + RD:P + 2 * RD]
        wc_h = keep["wc_h"][:, :].rearrange("p (m c) -> p m c", m=PAIRS)
        wc_l = keep["wc_l"][:, :].rearrange("p (m c) -> p m c", m=PAIRS)
        wqk_h = keep["wqk_h"][:, :].rearrange("p (k n) -> p k n", k=KT)
        wqk_l = keep["wqk_l"][:, :].rearrange("p (k n) -> p k n", k=KT)
        GN1 = 6
        UN = 1.0 / (LN_S * AW_S)
        lags = list(range(-1, TAIL + 1))
        block = ctx.enter_context(nc.Block())

        def reached(value, most):
            if isinstance(value, int):
                value = min(value, most)
                return value if value > 0 else None
            return value

        def need(eng, sem, value, most):
            value = reached(value, most)
            if value is not None:
                eng.wait_ge(sem, value)

        @block.sync
        def _(sp):
            def load(b):
                sp.dma_start(x_f[0:CI, PAD:PAD + T], x_d[bass.ds(b, 1), :, :].rearrange("a c t -> (a c) t")
                             ).then_inc(x_loaded, 16)
                sp.dma_start(x_f[CI:P, PAD - 1:PAD - 1 + T],
                             x_d[bass.ds(b, 1), :, :].rearrange("a c t -> (a c) t")).then_inc(x_loaded, 16)

            sp.wait_ge(zeroed_x, 1)
            load(0)
            with sp.Fori(1, B) as b:
                sp.wait_ge(x_hi, b)
                sp.wait_ge(x_lo, b)
                load(b)

        @block.scalar
        def _(act):
            def copy_y1(i, p, c):
                act.wait_ge(conv_done, i * 4 + (c + 1))
                if c == 0:
                    need(act, gelu1_done, i - 1, B)
                act.activation(y1[p][:, c * CHUNK:(c + 1) * CHUNK], conv_ps[c % 2][:, :], ACT.Copy
                               ).then_inc(y1_copied, 1)

            def hidden_high(b, hf):
                act.wait_ge(ht_done, b * 2 + (hf + 1))
                if hf == 0:
                    need(act, proj_done, b, B)
                act.activation(ht_h[:, hf * CHUNK:(hf + 1) * CHUNK], turn_ps[:, :], ACT.Copy,
                               scale=LN_S).then_inc(ht_hi, 1)

            def body(i, p, ok):
                if ok(0):
                    copy_y1(i, p, 0)
                if ok(TAIL):
                    b = i - TAIL
                    act.wait_ge(tail1_done, b + 1)
                    act.activation(keep["qct_h"][:, :, bass.ds(b * P, P)],
                                   turn_ps[:, 0:QR].rearrange("p (k n) -> p k n", k=QT),
                                   ACT.Copy, scale=QC_S).then_inc(t1_hi, 1)
                    act.activation(keep["kct_h"][:, bass.ds(b * P, P)], turn_ps[:, QR:QR + P],
                                   ACT.Copy, scale=KC_S).then_inc(t1_hi, 1)
                    act.activation(keep["kc_h"][:, bass.ds(b * P, P)], k_n[:, :], ACT.Copy, scale=KC_S
                                   ).then_inc(kc_hi, 1)
                if ok(-1):
                    act.wait_ge(x_loaded, i * 32 + 64)
                    need(act, conv_done, i * 4, 4 * B)
                    act.activation(x_h[1 - p][:, :], x_f[:, :], ACT.Copy).then_inc(x_hi, 1)
                if ok(0):
                    copy_y1(i, p, 1)
                if ok(TAIL):
                    b = i - TAIL
                    act.wait_ge(tail2_done, b + 1)
                    act.activation(keep["kr_h"][:, bass.ds(b * P, P)], turn_ps[:, 0:P], ACT.Copy,
                                   scale=KR_S * UN).then_inc(t2_hi, 1)
                if ok(0):
                    copy_y1(i, p, 2)
                if ok(PROJ):
                    hidden_high(i - PROJ, 0)
                if ok(GELU1):
                    act.wait_ge(norm_step, (i - 1) * NORM_STEPS + GN_STEPS)
                    need(act, dw_step, (i - DW + 1) * DW_TAPS, B * DW_TAPS)
                    act.activation(g1[:, DW_PAD:DW_PAD + T], y1[1 - p][:, :], ACT.Gelu, bias=c12[:, 1:2],
                                   scale=c12[:, 0:1]).then_inc(gelu1_done, 1)
                if ok(DW):
                    b = i - DW
                    act.wait_ge(dw_step, b * DW_TAPS + DW_TAPS)
                    need(act, pw_done, b * 2, 2 * B)
                    act.activation(dw_h[:, :], dw[:, :], ACT.Copy, scale=DW_S).then_inc(dw_hi, 1)
                if ok(0):
                    copy_y1(i, p, 3)
                if ok(PROJ):
                    hidden_high(i - PROJ, 1)
                if ok(GELU2):
                    b = i - GELU2
                    act.wait_ge(norm_step, (i - 1) * NORM_STEPS + GN_STEPS)
                    for hf in range(2):
                        act.activation(resid[:, bass.ds(b * D + hf * CHUNK, CHUNK)], pw_ps[hf][:, :],
                                       ACT.Gelu, bias=c12[:, 3:4], scale=c12[:, 2:3]).then_inc(gelu2_done, 1)
                if ok(HID):
                    b = i - HID
                    act.wait_ge(norm_step, (i - 1) * NORM_STEPS + LN_STEPS)
                    need(act, ht_done, b * 2, 2 * B)
                    act.activation(hid[:, :], resid[:, bass.ds(b * D, D)], ACT.Identity, bias=c3[:, 1:2],
                                   scale=c3[:, 0:1]).then_inc(hid_done, 1)
                if ok(PROJ):
                    b = i - PROJ
                    act.wait_ge(proj_done, b + 1)
                    act.wait_ge(norm_step, i * NORM_STEPS)
                    act.activation(junk[:, :], q_ps[:, 0:QR], ACT.Square, scale=UN * QR ** -0.5,
                                   accum_out=ss[:, 0:1]).then_inc(ss_done, 1)
                    act.wait_ge(ss_done, b * 2 + 1)
                    act.activation(junk[:, 0:KVR], kv_ps[:, 0:KVR], ACT.Square, scale=UN * KVR ** -0.5,
                                   accum_out=ss[:, 1:2]).then_inc(ss_done, 1)

            act.wait_ge(zeroed, 5)
            pipeline(act, body, -1, lags, TAIL)

        @block.gpsimd
        def _(pool):
            pool.memset(g1[:, 0:DW_PAD], 0.0).then_inc(zeroed, 1)
            pool.memset(g1[:, DW_PAD + T:], 0.0).then_inc(zeroed, 1)
            pool.memset(st[:, :], 1.0).then_inc(zeroed, 1)
            pool.memset(st3[:, :], 1.0).then_inc(zeroed, 1)
            pool.memset(ss[:, :], 1.0).then_inc(zeroed, 1)

            def norms(i):
                waits = ((s_copied, reached(i, LAST + GELU2)), (ln_step, reached((i - HID) * 3 + 3, 3 * B)),
                         (ss_done, reached((i - NORM) * 2 + 2, 2 * B)))
                wait_apart(pool, pool_passed, *((c, n) for c, n in waits if n is not None))
                link = Chain(pool, norm_step, i - 1, NORM_STEPS, pool_passed)
                mean, sq = s[:, 0:4:2], s[:, 1:4:2]
                link(pool.tensor_tensor(msq[:, :], mean, mean, ALU.mult), apart=False)
                link(pool.tensor_scalar(v[:, 2:3], st3[:, 1:2], LN_EPS, None, ALU.add), apart=False)
                link(pool.tensor_scalar(v[:, 3:5], ss[:, :], 1e-30, None, ALU.max))
                link(pool.tensor_tensor(msq[:, :], sq, msq[:, :], ALU.subtract))
                link(pool.tensor_scalar(v[:, 0:2], msq[:, :], 0.0, GN_EPS * GN_SCALE ** 2, ALU.max, ALU.add))
                link(pool.tensor_scalar(vm[:, :], v[:, :], -0.5, None, ALU.mult), apart=False)
                link(pool.tensor_scalar(y[:, :].bitcast(I32), v[:, :].bitcast(I32), -0.5, RSQRT_MAGIC,
                                        ALU.mult, ALU.add))
                for _ in range(3):
                    link(pool.tensor_tensor(t[:, :], y[:, :], y[:, :], ALU.mult))
                    link(pool.tensor_tensor(t[:, :], t[:, :], vm[:, :], ALU.mult))
                    link(pool.tensor_scalar(t[:, :], t[:, :], 1.5, None, ALU.add))
                    link(pool.tensor_tensor(y[:, :], y[:, :], t[:, :], ALU.mult))
                waits = ((gelu1_done, reached(i - GELU1, B)), (gelu2_done, reached((i - GELU2) * 2, 2 * B)),
                         (hid_done, reached(i - HID, B)), (rinv_done, reached(i - NORM, B)))
                wait_apart(pool, pool_passed, *((c, n) for c, n in waits if n is not None))
                scale, bias = c12[:, 0:4:2], c12[:, 1:4:2]
                link(pool.tensor_tensor(scale, y[:, 0:2], params[:, GN1:GN1 + 4:2], ALU.mult), apart=False)
                link(pool.tensor_tensor(c3[:, 1:2], st3[:, 0:1], y[:, 2:3], ALU.mult))
                link(pool.tensor_tensor(msq[:, :], mean, scale, ALU.mult))
                link(pool.tensor_tensor(bias, params[:, GN1 + 1:GN1 + 4:2], msq[:, :], ALU.subtract),
                     apart=False)
                assert link.n == GN_STEPS
                link(pool.tensor_scalar(c3[:, 1:2], c3[:, 1:2], -1.0, None, ALU.mult), apart=False)
                link(pool.tensor_scalar(c3[:, 0:1], y[:, 2:3], 1.0, None, ALU.mult), apart=False)
                assert link.n == LN_STEPS
                link(pool.tensor_tensor(nrm[:, :], v[:, 3:5], y[:, 3:5], ALU.mult))
                link(pool.tensor_scalar(nrm[:, :], nrm[:, :], RMS_EPS, None, ALU.add))
                link(pool.tensor_scalar(nrm[:, :], nrm[:, :], LN_S * AW_S, None, ALU.mult))
                assert link.n == NORM_STEPS

            def body(i, p, ok):
                if not isinstance(i, int) or 1 <= i <= LAST + NORM:
                    norms(i)
                if ok(-1):
                    wait_apart(pool, pool_passed, (x_hi, i + 2))
                    pool.tensor_tensor(x_l[1 - p][:, :], x_f[:, :], x_h[1 - p][:, :], ALU.subtract
                                       ).then_inc(x_lo, 1)

            pool.wait_ge(zeroed, 5)
            pipeline(pool, body, -1, lags, TAIL)

        @block.vector
        def _(dve):
            dve.memset(x_f[:, :], 0.0).then_inc(zeroed_x, 1)

            def low(out, src, scale, high, done):
                dve.scalar_tensor_tensor(out=out, in0=src, scalar=scale, in1=high, op0=ALU.mult,
                                         op1=ALU.subtract).then_inc(done, 1)

            def stats1(i, p, c):
                dve.wait_ge(y1_copied, i * 4 + (c + 1))
                dve.bn_stats(bn1[:, c, :], y1[p][:, c * CHUNK:(c + 1) * CHUNK]).then_inc(bn1_done, 1)

            def mean_and_square(ready, b, out, bn):
                link = Chain(dve, ready, b, 2)
                link(dve.bn_aggr(out, bn))
                link(dve.scalar_tensor_tensor(out=out[:, 1:2], in0=out[:, 0:1], scalar=out[:, 0:1],
                                              in1=out[:, 1:2], op0=ALU.mult, op1=ALU.add))

            def tap(b, k):
                if k == 0:
                    dve.wait_ge(gelu1_done, b + 1)
                    need(dve, dw_hi, b, B)
                    dve.tensor_scalar(dw[:, :], g1[:, 0:2 * D:2], params[:, 0:1], params[:, 5:6],
                                      ALU.mult, ALU.add).then_inc(dw_step, 1)
                else:
                    dve.wait_ge(dw_step, b * DW_TAPS + k)
                    dve.scalar_tensor_tensor(out=dw[:, :], in0=g1[:, k:k + 2 * D - 1:2],
                                             scalar=params[:, k:k + 1], in1=dw[:, :],
                                             op0=ALU.mult, op1=ALU.add).then_inc(dw_step, 1)

            def hidden_low(b, hf):
                dve.wait_ge(ht_hi, b * 2 + (hf + 1))
                sl = slice(hf * CHUNK, (hf + 1) * CHUNK)
                low(ht_l[:, sl], turn_ps[:, :], LN_S, ht_h[:, sl], ht_lo)

            def latent_norms(i, b):
                dve.wait_ge(norm_step, i * NORM_STEPS)
                dve.reciprocal(rinv[:, :], nrm[:, :]).then_inc(rinv_done, 1)
                HR = RD // 2
                dve.tensor_tensor(kr_a[:, :], kv_ps[:, KVR:KVR + RD], cos, ALU.mult).then_inc(kr_step, 1)
                dve.tensor_tensor(kr_b[:, 0:HR], kv_ps[:, KVR + HR:KVR + RD], sin[:, 0:HR], ALU.mult
                                  ).then_inc(kr_step, 1)
                dve.tensor_tensor(kr_b[:, HR:RD], kv_ps[:, KVR:KVR + HR], sin[:, HR:RD], ALU.mult
                                  ).then_inc(kr_step, 1)
                dve.wait_ge(rinv_done, b + 1)
                need(dve, tail1_done, b, B)
                need(dve, kc_lo, b, B)
                dve.scalar_tensor_tensor(out=q_n[:, :], in0=q_ps[:, 0:QR], scalar=rinv[:, 0:1],
                                         in1=gains[:, 0:QR], op0=ALU.mult, op1=ALU.mult
                                         ).then_inc(qn_done, 1)
                dve.scalar_tensor_tensor(out=k_n[:, :], in0=kv_ps[:, 0:KVR], scalar=rinv[:, 1:2],
                                         in1=gains[:, QR:QR + KVR], op0=ALU.mult, op1=ALU.mult
                                         ).then_inc(kn_done, 1)
                dve.wait_ge(kr_step, b * 5 + 3)
                need(dve, tail2_done, b, B)
                for half in range(2):
                    dve.tensor_tensor(kr2[:, half * RD:(half + 1) * RD], kr_a[:, :], kr_b[:, :], ALU.add
                                      ).then_inc(kr_step, 1)

            def body(i, p, ok):
                if ok(GELU1) or ok(GELU2):
                    dve.wait_ge(stat_done, i)
                    need(dve, norm_step, (i - 1) * NORM_STEPS, (LAST + NORM) * NORM_STEPS)
                    dve.tensor_copy(s[:, :], stat_ps[:, 0:4]).then_inc(s_copied, 1)
                if ok(DW):
                    tap(i - DW, 0)
                if ok(TAIL):
                    b = i - TAIL
                    dve.wait_ge(t1_hi, b * 2 + 2)
                    low(keep["qct_l"][:, :, bass.ds(b * P, P)],
                        turn_ps[:, 0:QR].rearrange("p (k n) -> p k n", k=QT), QC_S,
                        keep["qct_h"][:, :, bass.ds(b * P, P)], t1_lo)
                    low(keep["kct_l"][:, bass.ds(b * P, P)], turn_ps[:, QR:QR + P], KC_S,
                        keep["kct_h"][:, bass.ds(b * P, P)], t1_lo)
                    dve.wait_ge(kc_hi, b + 1)
                    low(keep["kc_l"][:, bass.ds(b * P, P)], k_n[:, :], KC_S,
                        keep["kc_h"][:, bass.ds(b * P, P)], kc_lo)
                if ok(DW):
                    tap(i - DW, 1)
                if ok(0):
                    stats1(i, p, 0)
                if ok(DW):
                    tap(i - DW, 2)
                if ok(TAIL):
                    b = i - TAIL
                    dve.wait_ge(t2_hi, b + 1)
                    low(keep["kr_l"][:, bass.ds(b * P, P)], turn_ps[:, 0:P], KR_S * UN,
                        keep["kr_h"][:, bass.ds(b * P, P)], t2_lo)
                if ok(DW):
                    tap(i - DW, 3)
                if ok(0):
                    stats1(i, p, 1)
                if ok(DW):
                    tap(i - DW, 4)
                if ok(PROJ):
                    hidden_low(i - PROJ, 0)
                if ok(NORM):
                    latent_norms(i, i - NORM)
                if ok(0):
                    stats1(i, p, 2)
                if ok(DW):
                    b = i - DW
                    dve.wait_ge(dw_hi, b + 1)
                    need(dve, pw_done, b * 2, 2 * B)
                    low(dw_l[:, :], dw[:, :], DW_S, dw_h[:, :], dw_lo)
                if ok(PROJ):
                    hidden_low(i - PROJ, 1)
                if ok(0):
                    stats1(i, p, 3)
                    waits = [(bn1_done, i * 4 + 4)]
                    if not isinstance(i, int) or i >= 1:
                        waits.append((stat_done, i))
                    wait_apart(dve, dve_passed, *waits)
                    mean_and_square(st1_ready, i, st[:, 0:2], bn1[:, :, :])
                if ok(GELU2):
                    b = i - GELU2
                    dve.wait_ge(gelu2_done, b * 2 + 2)
                    for hf in range(2):
                        dve.bn_stats(bn3[:, hf, :], resid[:, bass.ds(b * D + hf * CHUNK, CHUNK)]
                                     ).then_inc(ln_step, 1)
                    wait_apart(dve, dve_passed, (ln_step, b * 3 + 2), (norm_step, i * NORM_STEPS))
                    dve.bn_aggr(st3[:, :], bn3[:, :, :]).then_inc(ln_step, 1)
                if ok(DW):
                    b = i - DW
                    for hf in range(2):
                        dve.wait_ge(pw_done, b * 2 + (hf + 1))
                        dve.bn_stats(bn2[:, hf, :], pw_ps[hf][:, :]).then_inc(bn2_done, 1)
                    wait_apart(dve, dve_passed, (bn2_done, b * 2 + 2), (stat_done, i))
                    mean_and_square(st2_ready, b, st[:, 2:4], bn2[:, :, :])

            dve.wait_ge(zeroed, 5)
            pipeline(dve, body, -1, lags, TAIL)

        @block.tensor
        def _(pe):
            def conv(i, p, c):
                if c == 0:
                    pe.wait_ge(x_lo, i + 1)
                need(pe, y1_copied, i * 4 + (c - 1), 4 * B)
                n = 0
                for w, x in ((wc_h, x_h), (wc_l, x_h), (wc_h, x_l)):
                    for m in range(PAIRS):
                        lo = c * CHUNK + 2 * m
                        last = pe.matmul(conv_ps[c % 2][:, :], w[:, m, :], x[p][:, lo:lo + CHUNK],
                                         start=n == 0, stop=n == 3 * PAIRS - 1)
                        n += 1
                last.then_inc(conv_done, 1)

            def turn_hidden(i, hf):
                b = i - PROJ
                if hf == 0:
                    pe.wait_ge(hid_done, b + 1)
                    need(pe, t2_lo, i - TAIL + 1, B)
                need(pe, ht_lo, b * 2 + hf, 2 * B)
                for k in range(4):
                    last = pe.transpose(turn_ps[:, k * P:(k + 1) * P],
                                        hid[:, (4 * hf + k) * P:(4 * hf + k + 1) * P], ident)
                last.then_inc(ht_done, 1)

            def pointwise(i):
                b = i - DW
                pe.wait_ge(dw_lo, b + 1)
                need(pe, gelu2_done, b * 2, 2 * B)
                for hf in range(2):
                    sl = slice(hf * CHUNK, (hf + 1) * CHUNK)
                    pe.matmul(pw_ps[hf][:, :], keep["pw_h"][:, :], dw_h[:, sl], start=True, stop=False)
                    pe.matmul(pw_ps[hf][:, :], keep["pw_l"][:, :], dw_h[:, sl], start=False, stop=False)
                    pe.matmul(pw_ps[hf][:, :], keep["pw_h"][:, :], dw_l[:, sl], start=False, stop=True
                              ).then_inc(pw_done, 1)

            def project(i):
                b = i - PROJ
                need(pe, kr_step, b * 5, 5 * B)
                need(pe, qn_done, b, B)
                need(pe, kn_done, b, B)
                for k in range(KT):
                    if k % 4 == 0:
                        pe.wait_ge(ht_lo, b * 2 + (k // 4 + 1))
                    for n, (h, w) in enumerate(((ht_h, wqk_h), (ht_h, wqk_l), (ht_l, wqk_h))):
                        lhs = h[:, k * P:(k + 1) * P]
                        first, end = k == 0 and n == 0, k == KT - 1 and n == 2
                        pe.matmul(q_ps[:, 0:QR], lhs, w[:, k, 0:QR], start=first, stop=end)
                        last = pe.matmul(kv_ps[:, 0:KVR + RD], lhs, w[:, k, QR:QR + KVR + RD],
                                         start=first, stop=end)
                last.then_inc(proj_done, 1)

            def body(i, p, ok):
                if ok(0):
                    conv(i, p, 0)
                if ok(GELU1) or ok(GELU2):
                    need(pe, st1_ready, i * 2, 2 * B)
                    need(pe, st2_ready, (i - GELU2) * 2 + 2, 2 * B)
                    need(pe, s_copied, i - 1, LAST + GELU2)
                    pe.matmul(stat_ps[:, 0:4], keep["mean_mat"][:, :], st[:, :], start=True, stop=True
                              ).then_inc(stat_done, 1)
                if ok(TAIL):
                    b = i - TAIL
                    pe.wait_ge(qn_done, b + 1)
                    pe.wait_ge(kn_done, b + 1)
                    need(pe, ht_lo, b * 2 + 4, 2 * B)
                    for k in range(QT):
                        pe.transpose(turn_ps[:, k * P:(k + 1) * P], q_n[:, k * P:(k + 1) * P], ident)
                    pe.transpose(turn_ps[:, QR:QR + P], k_n[:, :], ident).then_inc(tail1_done, 1)
                if ok(0):
                    conv(i, p, 1)
                if ok(TAIL):
                    b = i - TAIL
                    pe.wait_ge(kr_step, b * 5 + 5)
                    pe.wait_ge(t1_lo, b * 2 + 2)
                    pe.transpose(turn_ps[:, 0:P], kr2[:, :], ident).then_inc(tail2_done, 1)
                if ok(0):
                    conv(i, p, 2)
                if ok(PROJ):
                    turn_hidden(i, 0)
                if ok(0):
                    conv(i, p, 3)
                if ok(PROJ):
                    turn_hidden(i, 1)
                    project(i)
                if ok(DW):
                    pointwise(i)

            pe.wait_ge(zeroed, 5)
            pipeline(pe, body, 0, lags, TAIL)


def fresh(eng, value, most):
    if isinstance(value, int):
        return value
    register = eng.alloc_register(None)
    eng.reg_mov(register, value)
    return eng.snap(register, min_val=0, max_val=most)


class Round:

    def __init__(self, eng, t, parity=None):
        self.eng, self.t, self.known, self.kept = eng, t, isinstance(t, int), {}
        self.parity = t % 2 if self.known else parity

    def held(self, name, value, most):
        if name not in self.kept:
            self.kept[name] = fresh(self.eng, value, most)
        return self.kept[name]

    @property
    def slot(self):
        return self.held("slot", self.t * QUAD, ROUNDS * QUAD)

    @property
    def group(self):
        return self.held("group", self.t // QUADS, GROUPS)

    @property
    def side(self):
        return self.held("side", (self.t // QUADS) % 2, 1)

    @property
    def tok(self):
        return self.held("tok", (self.t % QUADS) * (QUAD * P), TOK - QUAD * P)

    @property
    def half(self):
        if self.parity is not None:
            return self.parity * (HEADS * CHUNK)
        return self.held("half", (self.t % 2) * (HEADS * CHUNK), HEADS * CHUNK)

    @property
    def place(self):
        return self.held("place", self.t % HEADS, HEADS - 1)


def attention_phase(nc, keep, heads_d):
    with ExitStack() as ctx:
        def sb(name, shape, dt=F32):
            return ctx.enter_context(nc.sbuf_tensor(name, shape, dt))

        def pb(name, dt=F32):
            return ctx.enter_context(nc.psum_tensor(name, [P, CHUNK], dt))

        def sem(name):
            return ctx.enter_context(nc.semaphore(name))

        raw = sb("raw", [P, RAW])
        wp_h, wp_l = sb("wp_h", [P, 2, QT, HEADS, P], F16), sb("wp_l", [P, 2, QT, HEADS, P], F16)
        wr_h, wr_l = sb("wr_h", [P, 2, QT, HEADS * RD], F16), sb("wr_l", [P, 2, QT, HEADS * RD], F16)
        m_h, m_l = sb("m_h", [P, 2 * HEADS * D], F16), sb("m_l", [P, 2 * HEADS * D], F16)
        qp_h, qp_l = sb("qp_h", [P, 2 * HEADS * CHUNK], F16), sb("qp_l", [P, 2 * HEADS * CHUNK], F16)
        ra, rb, rz = (sb(n, [P, HEADS, RD]) for n in ("ra", "rb", "rz"))
        z = sb("z", [P, HEADS, 2 * RD], F16)
        zt = sb("zt", [P, HEADS, P], F16)
        prob = sb("prob", [P, HEADS, P])
        pt_h, pt_l = sb("pt_h", [P, CHUNK], F16), sb("pt_l", [P, CHUNK], F16)
        ot_h, ot_l = sb("ot_h", [P, HEADS, P], F16), sb("ot_l", [P, HEADS, P], F16)
        mx, nmx, rsum, rrec = (sb(n, [P, HEADS]) for n in ("mx", "nmx", "rsum", "rrec"))
        qp_ps, prod_ps, rope_ps, zt_ps = pb("qp_ps"), pb("prod_ps"), pb("rope_ps"), pb("zt_ps", F16)
        s_ps, pt_ps, out_ps = pb("s_ps"), pb("pt_ps"), [pb("out_ps0"), pb("out_ps1")]
        (raw_loaded, prod_done, prod_hi, prod_lo, wr_hi, wr_lo, qp_done, qp_hi, qp_lo, rope_done, rot_step,
         z_hi, z_lo, zt_done, zt_copied, s_done, max_step, exp_done, norm_step, pt_done, pt_hi, pt_lo,
         av_done, o_hi, o_lo, out_done, out_added) = (sem(n) for n in (
             "raw_loaded prod_done prod_hi prod_lo wr_hi wr_lo qp_done qp_hi qp_lo rope_done rot_step "
             "z_hi z_lo zt_done zt_copied s_done max_step exp_done norm_step pt_done pt_hi pt_lo "
             "av_done o_hi o_lo out_done out_added").split())
        resid, ident, ident_h = keep["resid"], keep["consts"][:, 0:P], keep["ident_h"]
        cos, sin = keep["consts"][:, P:P + RD], keep["consts"][:, P + RD:P + 2 * RD]
        qct_h, qct_l, kct_h, kct_l = keep["qct_h"], keep["qct_l"], keep["kct_h"], keep["kct_l"]
        kc_h, kc_l, kr_h, kr_l = keep["kc_h"], keep["kc_l"], keep["kr_h"], keep["kr_l"]
        EXP_SCALE = QK ** -0.5 / (QP_S * KC_S)
        block = ctx.enter_context(nc.Block())

        def rounds(eng, start, body):
            def run(t, more, parity=None):
                def at(k):
                    if isinstance(t, int) and not 0 <= t + k < ROUNDS:
                        return None
                    return Round(eng, t + k if k else t, parity if k == 0 or parity is None else 1 - parity)

                body(at(-1), at(0), at(1), more)

            start()
            run(0, True)
            with eng.Fori(1, ROUNDS - HEADS - 2, 2) as t:
                run(t, True, 1)
                run(t + 1, True, 0)
            run(ROUNDS - HEADS - 1, True)
            with eng.Fori(ROUNDS - HEADS, ROUNDS - 1) as t:
                run(t, False)
            run(ROUNDS - 1, False)

        @block.sync
        def _(sp):
            def load(h):
                sp.dma_start(raw[:, :], heads_d[bass.ds(h, 1), :, :].rearrange("a p n -> (a p) n")
                             ).then_inc(raw_loaded, 16)

            load(0)
            with sp.Fori(1, NH) as h:
                sp.wait_ge(prod_done, h * 3)
                sp.wait_ge(wr_lo, h)
                load(h)

        @block.scalar
        def _(act):
            def high(out, src, scale, done):
                act.activation(out, src, ACT.Copy, scale=scale).then_inc(done, 1)

            def prod_high(h, sd, k, part, fresh):
                act.wait_ge(prod_done, h * 3 + part + 1)
                if part == 0:
                    high(wp_h[:, bass.ds(sd, 1), :, bass.ds(k, 1), :].rearrange("p a t k n -> p (a t) (k n)"),
                         prod_ps[:, 0:QR].rearrange("p (t n) -> p t n", t=QT), WP_S, prod_hi)
                    if not fresh:
                        act.wait_ge(rope_done, h * 4 - 15)
                    high(wr_h[:, bass.ds(sd, 1), :, bass.ds(k * RD, RD)].rearrange("p a t n -> p (a t) n"),
                         raw[:, RAW_R:].rearrange("p (t n) -> p t n", t=QT), WR_S, wr_hi)
                else:
                    if not fresh:
                        act.wait_ge(out_done, h * 8 - 31)
                    high(m_h[:, bass.ds((sd * HEADS + k) * D + (part - 1) * CHUNK, CHUNK)], prod_ps[:, :],
                         M_S, prod_hi)

            def query_high(r, j):
                act.wait_ge(qp_done, r.slot + (j + 1))
                if not r.known or r.t >= 2:
                    act.wait_ge(s_done, r.slot - 4)
                high(qp_h[:, bass.ds(r.half + j * CHUNK, CHUNK)], qp_ps[:, :],
                     QP_S / (QC_S * WP_S), qp_hi)

            def rope_high(s):
                act.wait_ge(rot_step, s * 4 + 4)
                if not isinstance(s, int) or s >= 1:
                    act.wait_ge(zt_done, s)
                high(z[:, :, 0:RD], rz[:, :, :], QRO_S / (QC_S * WR_S), z_hi)

            def rope_copy(s):
                act.wait_ge(zt_done, s + 1)
                if not isinstance(s, int) or s >= 1:
                    act.wait_ge(s_done, s)
                act.activation(zt[:, :, :].rearrange("p h n -> p (h n)"), zt_ps[:, :], ACT.Copy
                               ).then_inc(zt_copied, 1)

            def start():
                for h in range(HEADS):
                    for part in range(3):
                        prod_high(h, 0, h, part, True)
                rope_high(0)
                rope_copy(0)
                for j in range(HEADS):
                    query_high(Round(act, 0), j)

            def body(before, now, after, more):
                for j in range(QUAD):
                    s = now.slot + j
                    act.wait_ge(max_step, s * 2 + 2)
                    if before or j:
                        act.wait_ge(pt_done, s)
                    for h in range(HEADS):
                        act.activation(prob[:, h, :], s_ps[:, h * P:(h + 1) * P], ACT.Exp,
                                       bias=nmx[:, h:h + 1], scale=EXP_SCALE,
                                       accum_out=rsum[:, h:h + 1]).then_inc(exp_done, 1)
                    if after or j < QUAD - 1:
                        rope_high(s + 1)
                    act.wait_ge(pt_done, s + 1)
                    if before or j:
                        act.wait_ge(av_done, s)
                    high(pt_h[:, :], pt_ps[:, :], PR_S, pt_hi)
                    if after:
                        query_high(after, j)
                    if after or j < QUAD - 1:
                        rope_copy(s + 1)
                    act.wait_ge(av_done, s + 1)
                    if before or j:
                        act.wait_ge(out_done, s * 2)
                    high(ot_h[:, :, :].rearrange("p h n -> p (h n)"), pt_ps[:, :], O_S / (PR_S * KC_S), o_hi)
                    if more and j:
                        prod_high(now.t + HEADS, now.side * -1 + 1, now.place, j - 1, False)

            rounds(act, start, body)

        @block.vector
        def _(dve):
            def low(out, src, scale, high, done):
                dve.scalar_tensor_tensor(out=out, in0=src, scalar=scale, in1=high, op0=ALU.mult,
                                         op1=ALU.subtract).then_inc(done, 1)

            def prod_low(h, sd, k, part):
                dve.wait_ge(prod_hi, h * 3 + part + 1)
                if part == 0:
                    at = (slice(None), bass.ds(sd, 1), slice(None), bass.ds(k, 1), slice(None))
                    low(wp_l[at].rearrange("p a t k n -> p (a t) (k n)"),
                        prod_ps[:, 0:QR].rearrange("p (t n) -> p t n", t=QT), WP_S,
                        wp_h[at].rearrange("p a t k n -> p (a t) (k n)"), prod_lo)
                    dve.wait_ge(wr_hi, h + 1)
                    at = (slice(None), bass.ds(sd, 1), slice(None), bass.ds(k * RD, RD))
                    low(wr_l[at].rearrange("p a t n -> p (a t) n"),
                        raw[:, RAW_R:].rearrange("p (t n) -> p t n", t=QT), WR_S,
                        wr_h[at].rearrange("p a t n -> p (a t) n"), wr_lo)
                else:
                    at = bass.ds((sd * HEADS + k) * D + (part - 1) * CHUNK, CHUNK)
                    low(m_l[:, at], prod_ps[:, :], M_S, m_h[:, at], prod_lo)

            def query_low(r, j):
                dve.wait_ge(qp_hi, r.slot + (j + 1))
                at = bass.ds(r.half + j * CHUNK, CHUNK)
                low(qp_l[:, at], qp_ps[:, :], QP_S / (QC_S * WP_S), qp_h[:, at], qp_lo)

            HR = RD // 2

            def rotate(s):
                dve.wait_ge(rope_done, s + 1)
                x = rope_ps[:, 0:HEADS * RD].rearrange("p (h n) -> p h n", h=HEADS)
                dve.tensor_tensor(ra[:, :, :], x, cos[:, None, :].broadcast_to([P, HEADS, RD]), ALU.mult
                                  ).then_inc(rot_step, 1)
                dve.tensor_tensor(rb[:, :, 0:HR], x[:, :, HR:RD],
                                  sin[:, None, 0:HR].broadcast_to([P, HEADS, HR]), ALU.mult
                                  ).then_inc(rot_step, 1)
                dve.tensor_tensor(rb[:, :, HR:RD], x[:, :, 0:HR],
                                  sin[:, None, HR:RD].broadcast_to([P, HEADS, HR]), ALU.mult
                                  ).then_inc(rot_step, 1)
                dve.wait_ge(rot_step, s * 4 + 3)
                if not isinstance(s, int) or s >= 1:
                    dve.wait_ge(z_hi, s)
                dve.tensor_tensor(rz[:, :, :], ra[:, :, :], rb[:, :, :], ALU.add).then_inc(rot_step, 1)

            def rope_low(s):
                dve.wait_ge(z_hi, s + 1)
                low(z[:, :, RD:2 * RD], rz[:, :, :], QRO_S / (QC_S * WR_S), z[:, :, 0:RD], z_lo)

            def add_out(r, j, hf):
                dve.wait_ge(out_done, r.slot * 2 + (j * 2 + hf + 1))
                at = bass.ds(r.tok * (D // P) + (j * D + hf * CHUNK), CHUNK)
                dve.scalar_tensor_tensor(out=resid[:, at], in0=out_ps[hf][:, :], scalar=1.0 / (O_S * M_S),
                                         in1=resid[:, at], op0=ALU.mult, op1=ALU.add).then_inc(out_added, 1)

            def start():
                for h in range(HEADS):
                    for part in range(3):
                        prod_low(h, 0, h, part)
                rotate(0)
                rope_low(0)
                for j in range(HEADS):
                    query_low(Round(dve, 0), j)

            def body(before, now, after, more):
                for j in range(QUAD):
                    s = now.slot + j
                    dve.wait_ge(s_done, s + 1)
                    dve.tensor_reduce(mx[:, :], s_ps[:, :].rearrange("p (h n) -> p h n", h=HEADS), AX.X,
                                      ALU.max).then_inc(max_step, 1)
                    dve.wait_ge(max_step, s * 2 + 1)
                    if before or j:
                        dve.wait_ge(exp_done, s * 4)
                    dve.tensor_scalar(nmx[:, :], mx[:, :], -EXP_SCALE, None, ALU.mult).then_inc(max_step, 1)
                    if after or j < QUAD - 1:
                        rotate(s + 1)
                    dve.wait_ge(exp_done, s * 4 + 4)
                    dve.reciprocal(rrec[:, :], rsum[:, :]).then_inc(norm_step, 1)
                    dve.wait_ge(norm_step, s * 2 + 1)
                    dve.tensor_tensor(prob[:, :, :], prob[:, :, :],
                                      rrec[:, :, None].broadcast_to([P, HEADS, P]), ALU.mult
                                      ).then_inc(norm_step, 1)
                    behind = (now, j - 1) if j else (before, QUAD - 1)
                    if behind[0]:
                        add_out(*behind, 0)
                    if after or j < QUAD - 1:
                        rope_low(s + 1)
                    if behind[0]:
                        add_out(*behind, 1)
                    dve.wait_ge(pt_hi, s + 1)
                    low(pt_l[:, :], pt_ps[:, :], PR_S, pt_h[:, :], pt_lo)
                    if after:
                        query_low(after, j)
                    dve.wait_ge(o_hi, s + 1)
                    low(ot_l[:, :, :].rearrange("p h n -> p (h n)"), pt_ps[:, :], O_S / (PR_S * KC_S),
                        ot_h[:, :, :].rearrange("p h n -> p (h n)"), o_lo)
                    if more and j:
                        prod_low(now.t + HEADS, now.side * -1 + 1, now.place, j - 1)
                if not after:
                    for hf in range(2):
                        add_out(now, QUAD - 1, hf)
                    dve.wait_ge(out_added, ROUNDS * 8)

            rounds(dve, start, body)

        @block.tensor
        def _(pe):
            def products(h, part):
                pe.wait_ge(raw_loaded, h * 16 + 16)
                if not isinstance(h, int) or h >= 1 or part:
                    pe.wait_ge(prod_lo, h * 3 + part)
                if part == 0:
                    for k in range(QT):
                        last = pe.matmul(prod_ps[:, k * P:(k + 1) * P], raw[:, RAW_Q + k * P:RAW_Q + (k + 1) * P],
                                         raw[:, RAW_K:RAW_K + P], start=True, stop=True)
                else:
                    at = RAW_O + (part - 1) * CHUNK
                    last = pe.matmul(prod_ps[:, :], raw[:, RAW_V:RAW_V + P], raw[:, at:at + CHUNK],
                                     start=True, stop=True)
                last.then_inc(prod_done, 1)

            def queries(r, j):
                pe.wait_ge(prod_lo, r.group * (3 * HEADS) + (3 * j + 1))
                if not r.known or r.t or j:
                    pe.wait_ge(qp_lo, r.slot + j)
                side, tok = fresh(pe, r.side, 1), fresh(pe, r.tok, TOK - QUAD * P)
                n = 0
                for w, q in ((wp_h, qct_h), (wp_l, qct_h), (wp_h, qct_l)):
                    for k in range(QT):
                        last = pe.matmul(qp_ps[:, :],
                                         w[:, bass.ds(side, 1), k, j, :].rearrange("p a n -> p (a n)"),
                                         q[:, k, bass.ds(tok, CHUNK)], start=n == 0, stop=n == 3 * QT - 1)
                        n += 1
                last.then_inc(qp_done, 1)

            def rope(r, j):
                if j == 0:
                    pe.wait_ge(wr_lo, r.group * HEADS + HEADS)
                if not r.known or r.t or j:
                    pe.wait_ge(rot_step, r.slot * 4 + (4 * j - 1))
                side, tok = fresh(pe, r.side, 1), fresh(pe, r.tok, TOK - QUAD * P)
                n = 0
                for q, w in ((qct_h, wr_h), (qct_h, wr_l), (qct_l, wr_h)):
                    for k in range(QT):
                        last = pe.matmul(rope_ps[:, 0:HEADS * RD], q[:, k, bass.ds(tok + j * P, P)],
                                         w[:, bass.ds(side, 1), k, :].rearrange("p a n -> p (a n)"),
                                         start=n == 0, stop=n == 3 * QT - 1)
                        n += 1
                last.then_inc(rope_done, 1)

            def turn_rope(s):
                pe.wait_ge(z_lo, s + 1)
                if not isinstance(s, int) or s >= 1:
                    pe.wait_ge(zt_copied, s)
                for h in range(HEADS):
                    last = pe.transpose(zt_ps[:, h * P:(h + 1) * P], z[:, h, :], ident_h[:, :])
                last.then_inc(zt_done, 1)

            def score_operands(r, j):
                keys = bass.ds(fresh(pe, r.tok, TOK - QUAD * P) + j * P, P)
                half = fresh(pe, r.half, HEADS * CHUNK)
                q = [bass.ds(half + (j * P + h * CHUNK), P) for h in range(HEADS)]
                operands = ([qp_h[:, at] for at in q], [qp_l[:, at] for at in q],
                            kct_h[:, keys], kct_l[:, keys], kr_h[:, keys], kr_l[:, keys])
                for ap in (*operands[2:], *operands[0], *operands[1]):
                    if not r.known:
                        pe.lower_ap(ap)
                return operands

            def scores(r, j, operands):
                q_h, q_l, k_h, k_l, rope_h, rope_l = operands
                if j == 0:
                    pe.wait_ge(qp_lo, r.slot + 4)
                if not r.known or r.t or j:
                    pe.wait_ge(exp_done, r.slot * 4 + 4 * j)
                out = [s_ps[:, h * P:(h + 1) * P] for h in range(HEADS)]
                for h in range(HEADS):
                    pe.matmul(out[h], q_h[h], k_h, start=h == 0, stop=False)
                    pe.matmul(out[h], q_h[h], k_l, start=False, stop=False)
                    pe.matmul(out[h], q_l[h], k_h, start=False, stop=False)
                pe.wait_ge(zt_copied, r.slot + (j + 1))
                for h in range(HEADS):
                    pe.matmul(out[h], zt[:, h, :], rope_h, start=False, stop=False)
                    last = pe.matmul(out[h], zt[:, h, :], rope_l, start=False, stop=h == HEADS - 1)
                last.then_inc(s_done, 1)

            def outputs(r, j):
                pe.wait_ge(o_lo, r.slot + (j + 1))
                if j == 0:
                    pe.wait_ge(prod_lo, r.group * (3 * HEADS) + 3 * HEADS)
                side = fresh(pe, r.side, 1)
                for hf in range(2):
                    if not r.known or r.t or j:
                        pe.wait_ge(out_added, r.slot * 2 + (j * 2 + hf - 1))
                    for h in range(HEADS):
                        at = bass.ds(side * (HEADS * D) + (h * D + hf * CHUNK), CHUNK)
                        pe.matmul(out_ps[hf][:, :], ot_h[:, h, :], m_h[:, at], start=h == 0, stop=False)
                        pe.matmul(out_ps[hf][:, :], ot_h[:, h, :], m_l[:, at], start=False, stop=False)
                        last = pe.matmul(out_ps[hf][:, :], ot_l[:, h, :], m_h[:, at], start=False,
                                         stop=h == HEADS - 1)
                    last.then_inc(out_done, 1)

            def start():
                for h in range(HEADS):
                    for part in range(3):
                        products(h, part)
                rope(Round(pe, 0), 0)
                turn_rope(0)
                for j in range(HEADS):
                    queries(Round(pe, 0), j)

            def body(before, now, after, more):
                operands = score_operands(now, 0)
                for j in range(QUAD):
                    s = now.slot + j
                    scores(now, j, operands)
                    if after or j < QUAD - 1:
                        if j < QUAD - 1:
                            rope(now, j + 1)
                        else:
                            rope(after, 0)
                    if before or j:
                        if j:
                            outputs(now, j - 1)
                        else:
                            outputs(before, QUAD - 1)
                    pe.wait_ge(norm_step, s * 2 + 2)
                    if before or j:
                        pe.wait_ge(o_lo, s)
                    for h in range(HEADS):
                        turned = pe.transpose(pt_ps[:, h * P:(h + 1) * P], prob[:, h, :], ident)
                    turned.then_inc(pt_done, 1)
                    if after:
                        queries(after, j)
                    if after or j < QUAD - 1:
                        turn_rope(s + 1)
                    if j < QUAD - 1:
                        operands = score_operands(now, j + 1)
                    pe.wait_ge(pt_lo, s + 1)
                    at = bass.ds(now.tok + j * P, P)
                    pe.matmul(pt_ps[:, :], kc_h[:, at], pt_h[:, :], start=True, stop=False)
                    pe.matmul(pt_ps[:, :], kc_l[:, at], pt_h[:, :], start=False, stop=False)
                    pe.matmul(pt_ps[:, :], kc_h[:, at], pt_l[:, :], start=False, stop=True).then_inc(av_done, 1)
                    if more and j:
                        products(now.t + HEADS, j - 1)
                if not after:
                    outputs(now, QUAD - 1)

            rounds(pe, start, body)


def ffn_phase(nc, keep, wb_d, ha_d, lb_d, bias_d, out_d):
    with ExitStack() as ctx:
        def sb(name, shape, dt=F32):
            return ctx.enter_context(nc.sbuf_tensor(name, shape, dt))

        def pb(name):
            return ctx.enter_context(nc.psum_tensor(name, [P, CHUNK], F32))

        def sem(name):
            return ctx.enter_context(nc.semaphore(name))

        stage = [sb(f"stage{i}", [P, D]) for i in range(2)]
        raw_ha, raw_lb = sb("raw_ha", [P, KT * HA]), sb("raw_lb", [P, D])
        wb_h, wb_l = sb("wb_h", [P, KT, D], F16), sb("wb_l", [P, KT, D], F16)
        ha_h, ha_l = sb("ha_h", [P, KT, HA], F16), sb("ha_l", [P, KT, HA], F16)
        lb_h, lb_l = sb("lb_h", [P, D], F16), sb("lb_l", [P, D], F16)
        bias = sb("bias", [P, D])
        hid = sb("hid2", [P, D])
        ht_h = [sb(f"fht_h{i}", [P, D], F16) for i in range(2)]
        ht_l = [sb(f"fht_l{i}", [P, D], F16) for i in range(2)]
        result = [sb(f"result{i}", [P, D]) for i in range(2)]
        bn, st, cf, v = sb("fbn", [P, 2, 6]), sb("fst", [P, 2]), sb("fcf", [P, 2]), sb("fv", [P, 3])
        logits = sb("logits", [P, 2 * NE])
        best = sb("best", [P, NE])
        taken = sb("taken", [P, NE])
        left, mask, ex, wsel, comb = (sb(n, [P, 2 * NE if n == "left" else NE])
                                      for n in ("left", "mask", "ex", "wsel", "comb"))
        nbest, wsum, wrec = sb("nbest", [P, 1]), sb("wsum", [P, 1]), sb("wrec", [P, 1])
        hw = sb("hw", [P, NE, RANK])
        hwt_h, hwt_l = sb("hwt_h", [P, P], F16), sb("hwt_l", [P, P], F16)
        turn_ps = [pb("fturn0"), pb("fturn1")]
        ha_ps, hwt_ps = pb("ha_ps"), pb("hwt_ps")
        out_ps = [[pb(f"fout{i}{j}") for j in range(2)] for i in range(2)]
        (pool_passed, dve_passed, filled, ln_step, coef, hid_done, biased, ht_done, ht_hi, ht_lo, ha_done, route_step, ex_done, hw_done,
         hwt_done, hwt_hi, hwt_lo, out_done, result_done, split_hi, split_lo, small_hi, small_lo) = (
            sem(n) for n in (
                "fpool_passed fdve_passed filled fln_step fcoef fhid_done biased fht_done fht_hi fht_lo ha_done route_step ex_done "
                "hw_done hwt_done hwt_hi hwt_lo fout_done result_done split_hi split_lo small_hi small_lo").split())
        stage_loaded = [sem(f"stage_loaded{i}") for i in range(2)]
        small_loaded = [sem(f"small_loaded{i}") for i in range(3)]
        stored = [sem(f"stored{i}") for i in range(2)]
        COEF = RSQRT_LINKS + 3
        ROUTE = 12
        resid, ident = keep["resid"], keep["consts"][:, 0:P]
        UN = 1.0 / (LN_S * AW_S)
        block = ctx.enter_context(nc.Block())

        @block.sync
        def _(sp):
            sp.dma_start(raw_ha[:, :], ha_d).then_inc(small_loaded[0], 16)
            sp.dma_start(raw_lb[:, :], lb_d).then_inc(small_loaded[1], 16)
            sp.dma_start(bias[:, :], bias_d.partition_broadcast(P)).then_inc(small_loaded[2], 16)
            for k in range(KT):
                if k >= 2:
                    sp.wait_ge(split_lo, k - 1)
                sp.dma_start(stage[k % 2][:, :], wb_d[:, k, :]).then_inc(stage_loaded[k % 2], 16)

            def store(b, p):
                sp.wait_ge(result_done, b * 2 + 2)
                sp.dma_start(out_d[bass.ds(b, 1), :, :].rearrange("a p n -> (a p) n"), result[p][:, :]
                             ).then_inc(stored[p], 16)

            with sp.Fori(0, B - 1, 2) as b:
                store(b, 0)
                store(b + 1, 1)
            for p in range(2):
                sp.wait_ge(stored[p], B // 2 * 16)

        @block.scalar
        def _(act):
            act.wait_ge(small_loaded[0], 16)
            act.activation(ha_h[:, :, :].rearrange("p k n -> p (k n)"), raw_ha[:, :], ACT.Copy, scale=AW_S
                           ).then_inc(small_hi, 1)
            act.wait_ge(small_loaded[1], 16)
            act.activation(lb_h[:, :], raw_lb[:, :], ACT.Copy, scale=LB_S).then_inc(small_hi, 1)
            for k in range(KT):
                act.wait_ge(stage_loaded[k % 2], 16 * (k // 2 + 1))
                act.activation(wb_h[:, k, :], stage[k % 2][:, :], ACT.Copy, scale=AW_S).then_inc(split_hi, 1)

            def body(i, p, ok):
                if ok(0):
                    act.wait_ge(route_step, i * ROUTE + 3)
                    act.activation(ex[:, :], logits[:, 0:NE], ACT.Exp, bias=nbest[:, 0:1], scale=UN
                                   ).then_inc(ex_done, 1)
                if ok(-1):
                    act.wait_ge(coef, i * COEF + 2 * COEF)
                    if not isinstance(i, int) or i >= 0:
                        act.wait_ge(ht_done, i * 2 + 2)
                    act.activation(hid[:, :], resid[:, bass.ds((i + 1) * D, D)], ACT.Identity,
                                   bias=cf[:, 1:2], scale=cf[:, 0:1]).then_inc(hid_done, 1)
                if ok(0):
                    act.wait_ge(hwt_done, i + 1)
                    if not isinstance(i, int) or i >= 1:
                        act.wait_ge(out_done, i * 2)
                    act.activation(hwt_h[:, :], hwt_ps[:, 0:P], ACT.Copy, scale=HW_S * UN).then_inc(hwt_hi, 1)
                if ok(-1):
                    for hf in range(2):
                        act.wait_ge(ht_done, i * 2 + hf + 3)
                        act.activation(ht_h[1 - p][:, hf * CHUNK:(hf + 1) * CHUNK], turn_ps[hf][:, :],
                                       ACT.Copy, scale=LN_S).then_inc(ht_hi, 1)

            pipeline(act, body, -1, [-1, 0], 2)

        @block.gpsimd
        def _(pool):
            def body(i, p, ok):
                if ok(0):
                    wait_apart(pool, pool_passed, (ln_step, i * 3 + 3))
                    link = Chain(pool, coef, i, COEF, pool_passed)
                    link(pool.tensor_scalar(v[:, 0:1], st[:, 1:2], LN_EPS, None, ALU.add))
                    newton_rsqrt(pool, link, cf[:, 0:1], v[:, 0:1], v[:, 1:2])
                    link(pool.tensor_scalar(v[:, 2:3], st[:, 0:1], -1.0, None, ALU.mult))
                    link(pool.tensor_tensor(cf[:, 1:2], v[:, 2:3], cf[:, 0:1], ALU.mult))
                    pool.wait_ge(hid_done, i + 1)
                    at = bass.ds(i * D, D)
                    pool.tensor_tensor(resid[:, at], resid[:, at], bias[:, :], ALU.add).then_inc(biased, 1)

            pool.wait_ge(small_loaded[2], 16)
            pipeline(pool, body, 0, [0], 2)

        @block.vector
        def _(dve):
            def low(out, src, scale, high, done):
                dve.scalar_tensor_tensor(out=out, in0=src, scalar=scale, in1=high, op0=ALU.mult,
                                         op1=ALU.subtract).then_inc(done, 1)

            dve.memset(logits[:, NE:], SENTINEL).then_inc(filled, 1)
            dve.memset(taken[:, :], SENTINEL).then_inc(filled, 1)

            def body(i, p, ok):
                later = not isinstance(i, int)
                if ok(-2):
                    if later or i >= -1:
                        dve.wait_ge(coef, (i + 2) * COEF)
                    for hf in range(2):
                        dve.bn_stats(bn[:, hf, :], resid[:, bass.ds((i + 2) * D + hf * CHUNK, CHUNK)]
                                     ).then_inc(ln_step, 1)
                    wait_apart(dve, dve_passed, (ln_step, (i + 2) * 3 + 2))
                    dve.bn_aggr(st[:, :], bn[:, :, :]).then_inc(ln_step, 1)
                if not later and i == -2:
                    low(ha_l[:, :, :].rearrange("p k n -> p (k n)"), raw_ha[:, :], AW_S,
                        ha_h[:, :, :].rearrange("p k n -> p (k n)"), small_lo)
                    low(lb_l[:, :], raw_lb[:, :], LB_S, lb_h[:, :], small_lo)
                    for k in range(KT):
                        dve.wait_ge(split_hi, k + 1)
                        low(wb_l[:, k, :], stage[k % 2][:, :], AW_S, wb_h[:, k, :], split_lo)
                if ok(0):
                    dve.wait_ge(ha_done, i + 1)
                    if later or i >= 1:
                        dve.wait_ge(ex_done, i)
                    link = Chain(dve, route_step, i, ROUTE, dve_passed)
                    link(dve.tensor_copy(logits[:, 0:NE], ha_ps[:, NE * RANK:HA]))
                    link(dve.max(best[:, :], logits[:, 0:NE]))
                    link(dve.tensor_scalar(nbest[:, :], best[:, 0:1], -UN, None, ALU.mult))
                    link(dve.tensor_copy(taken[:, 0:2], best[:, 0:2]))
                    link(dve.match_replace(left[:, :], taken[:, :], logits[:, :], SENTINEL))
                    link(dve.tensor_tensor(mask[:, :], left[:, 0:NE], logits[:, 0:NE], ALU.not_equal))
                    dve.wait_ge(ex_done, i + 1)
                    link(dve.tensor_tensor(wsel[:, :], ex[:, :], mask[:, :], ALU.mult))
                    link(dve.tensor_reduce(wsum[:, :], wsel[:, :], AX.X, ALU.add))
                    link(dve.reciprocal(wrec[:, :], wsum[:, :]))
                    link(dve.tensor_scalar(comb[:, :], wsel[:, :], wrec[:, 0:1], LORA_SCALE, ALU.mult, ALU.mult))
                    if later or i >= 1:
                        dve.wait_ge(hwt_done, i)
                    link(dve.tensor_tensor(hw[:, :, :],
                                           ha_ps[:, 0:NE * RANK].rearrange("p (e r) -> p e r", e=NE),
                                           comb[:, :, None].broadcast_to([P, NE, RANK]), ALU.mult))
                    dve.wait_ge(hwt_hi, i + 1)
                    link(dve.scalar_tensor_tensor(out=hwt_l[:, :], in0=hwt_ps[:, 0:P], scalar=HW_S * UN,
                                                  in1=hwt_h[:, :], op0=ALU.mult, op1=ALU.subtract))
                if ok(-1):
                    for hf in range(2):
                        dve.wait_ge(ht_hi, i * 2 + hf + 3)
                        sl = slice(hf * CHUNK, (hf + 1) * CHUNK)
                        low(ht_l[1 - p][:, sl], turn_ps[hf][:, :], LN_S, ht_h[1 - p][:, sl], ht_lo)
                if ok(0):
                    if later or i >= 2:
                        dve.wait_ge(stored[p], later_store(i, p))
                    dve.wait_ge(biased, i + 1)
                    for hf in range(2):
                        dve.wait_ge(out_done, i * 2 + hf + 1)
                        dve.scalar_tensor_tensor(out=result[p][:, hf * CHUNK:(hf + 1) * CHUNK],
                                                 in0=out_ps[p][hf][:, :], scalar=UN,
                                                 in1=resid[:, bass.ds(i * D + hf * CHUNK, CHUNK)],
                                                 op0=ALU.mult, op1=ALU.add).then_inc(result_done, 1)

            def later_store(i, p):
                return (i - p) * 8

            dve.wait_ge(filled, 2)
            dve.wait_ge(small_hi, 2)
            pipeline(dve, body, -2, [-2, -1, 0], 2)

        @block.tensor
        def _(pe):
            def body(i, p, ok):
                later = not isinstance(i, int)
                if ok(0):
                    pe.wait_ge(ht_lo, i * 2 + 2)
                    if later or i >= 1:
                        pe.wait_ge(route_step, i * ROUTE - 1)
                    n = 0
                    for k in range(KT):
                        for h, w in ((ht_h, ha_h), (ht_h, ha_l), (ht_l, ha_h)):
                            last = pe.matmul(ha_ps[:, 0:HA], h[p][:, k * P:(k + 1) * P], w[:, k, :],
                                             start=n == 0, stop=n == 3 * KT - 1)
                            n += 1
                    last.then_inc(ha_done, 1)
                    if later or i >= 2:
                        pe.wait_ge(result_done, i * 2 - 2)

                    def base(hf):
                        for k in range(KT):
                            if not later and i == 0 and hf == 0:
                                pe.wait_ge(split_lo, k + 1)
                            for n, (h, w) in enumerate(((ht_h, wb_h), (ht_h, wb_l), (ht_l, wb_h))):
                                pe.matmul(out_ps[p][hf][:, :], h[p][:, k * P:(k + 1) * P],
                                          w[:, k, hf * CHUNK:(hf + 1) * CHUNK],
                                          start=k == 0 and n == 0, stop=False)

                    base(0)
                    pe.wait_ge(route_step, i * ROUTE + 11)
                    pe.transpose(hwt_ps[:, 0:P], hw[:, :, :].rearrange("p e r -> p (e r)"), ident
                                 ).then_inc(hwt_done, 1)
                    base(1)
                if ok(-1):
                    pe.wait_ge(hid_done, i + 2)
                    for hf in range(2):
                        if later or i >= 0:
                            pe.wait_ge(ht_lo, i * 2 + hf + 1)
                        for k in range(4):
                            last = pe.transpose(turn_ps[hf][:, k * P:(k + 1) * P],
                                                hid[:, (4 * hf + k) * P:(4 * hf + k + 1) * P], ident)
                        last.then_inc(ht_done, 1)
                if ok(0):
                    pe.wait_ge(route_step, i * ROUTE + 12)
                    for hf in range(2):
                        sl = slice(hf * CHUNK, (hf + 1) * CHUNK)
                        pe.matmul(out_ps[p][hf][:, :], hwt_h[:, :], lb_h[:, sl], start=False, stop=False)
                        pe.matmul(out_ps[p][hf][:, :], hwt_h[:, :], lb_l[:, sl], start=False, stop=False)
                        pe.matmul(out_ps[p][hf][:, :], hwt_l[:, :], lb_h[:, sl], start=False, stop=True
                                  ).then_inc(out_done, 1)

            pe.wait_ge(small_lo, 2)
            pipeline(pe, body, -1, [-1, 0], 2)


def build(nc, x_d, wc_d, pw_d, wqk_d, rows_d, params_d, consts_d, heads_d, wb_d, ha_d, lb_d, bias_d, out_d):
    nc.disable_value_cache = True
    with ExitStack() as whole:
        def make(ctx, shapes):
            return {n: ctx.enter_context(nc.sbuf_tensor(n, list(s), dt)) for n, s, dt in shapes}

        keep = make(whole, [("resid", (P, B * D), F32), ("consts", (P, P + 2 * RD), F32),
                            ("ident_h", (P, P), F16), ("mean_mat", (P, P), F32)])
        with ExitStack() as first_two:
            latents = [("qct", (P, QT, TOK)), ("kct", (P, TOK)), ("kc", (P, TOK)), ("kr", (P, TOK))]
            keep.update(make(first_two, [(f"{n}_{part}", s, F16) for n, s in latents for part in "hl"]))
            with ExitStack() as first:
                keep.update(make(first, [
                    ("params", (P, 10), F32), ("gains", (P, QR + KVR), F32),
                    ("wc_h", (P, PAIRS * CH), F16), ("wc_l", (P, PAIRS * CH), F16),
                    ("pw_h", (P, CH), F16), ("pw_l", (P, CH), F16),
                    ("wqk_h", (P, KT * (QR + KVR + RD)), F16), ("wqk_l", (P, KT * (QR + KVR + RD)), F16)]))
                weights_stage(nc, keep, wc_d, wqk_d, pw_d, rows_d, params_d, consts_d)
                token_phase(nc, keep, x_d)
            nc.disable_value_cache = False
            attention_phase(nc, keep, heads_d)
            nc.disable_value_cache = True
        ffn_phase(nc, keep, wb_d, ha_d, lb_d, bias_d, out_d)


def rotary_tables(np):
    inv_freq = 1.0 / np.float32(10000.0) ** (np.arange(0, RD, 2, dtype=np.float32) / np.float32(RD))
    angles = np.outer(np.arange(CH, dtype=np.float32), inv_freq).astype(np.float32)
    c, s = np.cos(angles), np.sin(angles)
    return np.concatenate([c, c, -s, s], axis=1).astype(np.float32)


def kernel(**inputs):
    import numpy as np
    import concourse.bacc as bacc
    from concourse.bass_utils import run_bass_kernel_spmd

    a = {n.removeprefix("L0_"): np.asarray(v) for n, v in inputs.items()}
    taps = np.concatenate([a["tok_conv_in_w"], np.zeros((CH, CI, 1), np.float32)], axis=2)
    wc = taps.reshape(CH, CI, PAIRS, 2).transpose(3, 1, 2, 0).reshape(P, PAIRS * CH)
    wqk = np.concatenate([a["attn_w_qa"], a["attn_w_kva"]], axis=1)
    wqk = wqk.reshape(KT, P, QR + KVR + RD).transpose(1, 0, 2).reshape(P, -1)
    params = np.concatenate([a["tok_dw_w"][:, 0, :], np.stack([a[f"tok_{n}"] for n in (
        "dw_b", "gn1_w", "gn1_b", "gn2_w", "gn2_b")], axis=1)], axis=1)
    wqb = a["attn_w_qb"].reshape(QR, NH, QK)
    wkv = a["attn_w_kvb"].reshape(KVR, NH, 2, P)
    heads = np.concatenate([
        wqb[:, :, 0:P].transpose(1, 2, 0),
        wkv[:, :, 0].transpose(1, 2, 0), wkv[:, :, 1].transpose(1, 2, 0),
        a["attn_w_o"].reshape(NH, P, D),
        wqb[:, :, P:].reshape(QT, P, NH, RD).transpose(2, 1, 0, 3).reshape(NH, P, QT * RD)], axis=2)
    ha = np.concatenate([a["ffn_A"].reshape(NE * RANK, D), a["ffn_W_router"]], axis=0)
    arrays = {
        "x": a["x"], "wc": wc, "pw": a["tok_pw_w"][:, :, 0].T, "wqk": wqk,
        "rows": np.concatenate([a["attn_g_qa"], a["attn_g_kva"]]), "params": params,
        "consts": np.concatenate([np.eye(P, dtype=np.float32), rotary_tables(np)], axis=1),
        "heads": heads, "wb": a["ffn_W_base"].T.reshape(KT, P, D).transpose(1, 0, 2),
        "ha": ha.T.reshape(KT, P, HA).transpose(1, 0, 2).reshape(P, KT * HA),
        "lb": a["ffn_B"].transpose(0, 2, 1).reshape(NE * RANK, D), "bias": a["ffn_b_base"],
    }
    arrays = {f"{n}_in": np.ascontiguousarray(v) for n, v in arrays.items()}
    nc = bacc.Bacc("TRN2", target_bir_lowering=False, num_devices=1)
    args = [nc.dram_tensor(n, v.shape, mybir.dt.from_np(v.dtype), kind="ExternalInput").ap()
            for n, v in arrays.items()]
    args.append(nc.dram_tensor("tower_out", (B, CH, D), F32, kind="ExternalOutput").ap())
    build(nc, *args)
    ran = run_bass_kernel_spmd(nc, [arrays], core_ids=[0])
    return ran.results[0]["tower_out"]
```

```python
from contextlib import ExitStack

import concourse.bass as bass
from concourse import mybir

F32 = mybir.dt.float32
F16 = mybir.dt.float16
I32 = mybir.dt.int32
ALU = mybir.AluOpType
ACT = mybir.ActivationFunctionType
AX = mybir.AxisListType

B, CI, T, CH = 16, 64, 2048, 128
TAPS, PAD, DW_TAPS, DW_PAD = 7, 3, 5, 2
XW = T + 2 * PAD
PAIRS = (TAPS + 1) // 2
D = T // 2
P = 128
KT = D // P
QR, KVR, RD, NH = 384, 128, 64, 32
QT = QR // P
QK = RD + 128
TOK = B * CH
CHUNK = 512
HEADS = 4
GROUPS = NH // HEADS
QUAD = 4
QUADS = B // QUAD
ROUNDS = GROUPS * QUADS
RAW_Q, RAW_K, RAW_V, RAW_O, RAW_R = 0, QR, QR + P, QR + 2 * P, QR + 2 * P + D
RAW = RAW_R + QT * RD
NE, RANK = 8, 16
HA = NE * RANK + NE
GN_EPS, LN_EPS, RMS_EPS = 1e-5, 1e-5, 1e-6
LORA_SCALE = 2.0
RSQRT_MAGIC = float(0x5F3759DF)
SENTINEL = -3.0e38

CW_S = 2.0**12
DW_S, PW_S = 2.0**5, 2.0**7
LN_S, AW_S = 2.0**8, 2.0**8
QC_S, KC_S = 2.0**6, 2.0**6
KR_S, QRO_S = 2.0**7, 2.0**7
WP_S, WR_S, M_S = 2.0**9, 2.0**8, 2.0**10
QP_S = QC_S * WP_S / 2.0**7
PR_S = 2.0**12
O_S = 2.0**8
HW_S, LB_S = 2.0**8, 2.0**8
GN_SCALE = CW_S
assert GN_SCALE == DW_S * PW_S
assert QP_S * KC_S == KR_S * QRO_S
assert HW_S * LB_S == LN_S * AW_S


def pipeline(eng, body, first, lags, steady, unroll=2):
    assert steady >= max(lags)
    lo, hi = steady, B + min(lags)
    hi -= (hi - lo) % unroll
    for i in range(first, lo):
        body(i, i % 2, lambda lag, i=i: 0 <= i - lag < B)
    with eng.Fori(lo, hi - unroll + 1, unroll) as r:
        for u in range(unroll):
            body(r + u if u else r, (lo + u) % 2, lambda lag: True)
    for i in range(hi, B + max(lags)):
        body(i, i % 2, lambda lag, i=i: 0 <= i - lag < B)


def newton_rsqrt(pool, link, y, v, t):
    link(pool.tensor_scalar(y.bitcast(I32), v.bitcast(I32), -0.5, RSQRT_MAGIC, ALU.mult, ALU.add))
    for _ in range(3):
        link(pool.tensor_tensor(t, y, y, ALU.mult))
        link(pool.tensor_tensor(t, t, v, ALU.mult))
        link(pool.tensor_scalar(t, t, -0.5, 1.5, ALU.mult, ALU.add))
        link(pool.tensor_tensor(y, y, t, ALU.mult))


RSQRT_LINKS = 13


def wait_apart(eng, passed, *waits):
    for sem, value in waits:
        eng.wait_ge(sem, value)
    eng.sem_inc(passed, 1)


class Chain:

    def __init__(self, eng, sem, batch, per, passed=None):
        self.eng, self.sem, self.base, self.per, self.n = eng, sem, batch * per, per, 0
        self.passed = passed

    def __call__(self, ins, apart=True):
        self.n += 1
        assert self.n <= self.per
        ins.then_inc(self.sem, 1)
        if self.n < self.per and apart:
            if self.passed:
                wait_apart(self.eng, self.passed, (self.sem, self.base + self.n))
            else:
                self.eng.wait_ge(self.sem, self.base + self.n)


def token_phase(nc, keep, raw_loaded, x_d, wc_d, wqk_d, pw_d, rows_d, params_d, consts_d, heads_d):
    GELU1, DW, GELU2, HID, PROJ, NORM = 1, 2, 3, 4, 5, 6
    LAST = B - 1
    with ExitStack() as ctx:
        def sb(name, shape, dt=F32):
            return ctx.enter_context(nc.sbuf_tensor(name, shape, dt))

        def pb(name):
            return ctx.enter_context(nc.psum_tensor(name, [P, CHUNK], F32))

        def sem(name):
            return ctx.enter_context(nc.semaphore(name))

        x_f = keep["wide0"]
        x_h = [keep["wide1"][:, :].bitcast(F16)[:, i * XW:(i + 1) * XW] for i in range(2)]
        x_l = [sb(f"x_l{i}", [P, XW], F16) for i in range(2)]
        y1 = [sb(f"y1_{i}", [P, T]) for i in range(2)]
        g1 = sb("g1", [P, T + 2 * DW_PAD])
        dw = sb("dw", [P, D])
        dw_h, dw_l = sb("dw_h", [P, D], F16), sb("dw_l", [P, D], F16)
        hid = sb("hid", [P, D])
        ht_h, ht_l = sb("ht_h", [P, D], F16), sb("ht_l", [P, D], F16)
        q_g, k_g, k_n = sb("q_g", [P, QR]), sb("k_g", [P, KVR]), sb("k_n", [P, KVR])
        diag = sb("diag", [P, P])
        kr_a, kr_b, kr2 = sb("kr_a", [P, RD]), sb("kr_b", [P, RD]), sb("kr2", [P, 2 * RD])
        bn1, bn2, bn3 = sb("bn1", [P, 4, 6]), sb("bn2", [P, 2, 6]), sb("bn3", [P, 2, 6])
        st = sb("st", [P, 4])
        st3 = sb("st3", [P, 2])
        s = sb("s", [P, 4])
        msq = sb("msq", [P, 2])
        v, vm, y, t = (sb(n, [P, 5]) for n in ("v", "vm", "y", "t"))
        c12, c3 = sb("c12", [P, 4]), sb("c3", [P, 2])
        junk = sb("junk", [P, QR], F16)
        ss, nrm, rinv = sb("ss", [P, 2]), sb("nrm", [P, 2]), sb("rinv", [P, 2])
        conv_ps = [pb("conv_ps0"), pb("conv_ps1")]
        stat_ps, turn_ps = pb("stat_ps"), pb("turn_ps")
        pw_ps = [pb("pw_ps0"), pb("pw_ps1")]
        q_ps, kv_ps = pb("q_ps"), pb("kv_ps")
        raw = {n: keep["resid"][:, (B - 6) * D + at:(B - 6) * D + at + width] for n, at, width in (
            ("wc", 0, PAIRS * CH), ("pw", PAIRS * CH, CH), ("wqk", PAIRS * CH + CH, KT * (QR + KVR + RD)))}
        w_loaded = {n: sem(f"{n}_loaded") for n in ("wc", "pw", "wqk", "consts", "params", "gains")}
        w_hi, w_lo = {n: sem(f"{n}_hi") for n in raw}, {n: sem(f"{n}_lo") for n in raw}
        ident_done = sem("ident_done")
        quarter = KT * (QR + KVR + RD) // 4
        QUARTERS = [slice(k * quarter, (k + 1) * quarter) for k in range(4)]
        (pool_passed, dve_passed, zeroed, zeroed_x, x_loaded, x_hi, x_lo, conv_done, y1_copied, bn1_done,
         st1_ready, st2_ready, stat_done, s_copied, norm_step, gelu1_done, dw_step, dw_hi, dw_lo, pw_done,
         bn2_done, gelu2_done, ln_step, hid_done, ht_done, ht_hi, ht_lo, proj_done, ss_done, rinv_done,
         q_taken, diag_done, kn_done, kr_step, tail1_done, tail2_done, t1_hi, t1_lo, kc_hi, kc_lo, t2_hi,
         t2_lo) = (sem(n) for n in (
             "pool_passed dve_passed zeroed zeroed_x x_loaded x_hi x_lo conv_done y1_copied bn1_done "
             "st1_ready st2_ready stat_done s_copied norm_step gelu1_done dw_step dw_hi dw_lo pw_done "
             "bn2_done gelu2_done ln_step hid_done ht_done ht_hi ht_lo proj_done ss_done rinv_done "
             "q_taken diag_done kn_done kr_step tail1_done tail2_done t1_hi t1_lo kc_hi kc_lo t2_hi t2_lo").split())
        GN_STEPS, LN_STEPS, NORM_STEPS = 23, 25, 28
        params, gains, resid = keep["params"], keep["gains"], keep["resid"]
        ident = keep["consts"][:, 0:P]
        cos, sin = keep["consts"][:, P:P + RD], keep["consts"][:, P + RD:P + 2 * RD]
        wc_h = keep["wc_h"][:, :].rearrange("p (m c) -> p m c", m=PAIRS)
        wc_l = keep["wc_l"][:, :].rearrange("p (m c) -> p m c", m=PAIRS)
        wqk_h = keep["wqk_h"][:, :].rearrange("p (k n) -> p k n", k=KT)
        wqk_l = keep["wqk_l"][:, :].rearrange("p (k n) -> p k n", k=KT)
        GN1 = 6
        UN = 1.0 / (LN_S * AW_S)
        lags = list(range(-1, NORM + 1))
        block = ctx.enter_context(nc.Block())

        def reached(value, most):
            if isinstance(value, int):
                value = min(value, most)
                return value if value > 0 else None
            return value

        def need(eng, sem, value, most):
            value = reached(value, most)
            if value is not None:
                eng.wait_ge(sem, value)

        def wait_all(eng, passed, waits):
            waits = [(c, n) for c, n in waits if n is not None]
            if passed:
                wait_apart(eng, passed, *waits)
            else:
                for c, n in waits:
                    eng.wait_ge(c, n)

        def norms(eng, i, passed=None, between={}):
            waits = ((s_copied, reached(i, LAST + GELU2)), (ln_step, reached((i - HID) * 3 + 3, 3 * B)),
                     (ss_done, reached((i - NORM) * 2 + 2, 2 * B)))
            wait_all(eng, passed, waits)
            link = Chain(eng, norm_step, i - 1, NORM_STEPS, passed)
            mean, sq = s[:, 0:4:2], s[:, 1:4:2]
            link(eng.tensor_tensor(msq[:, :], mean, mean, ALU.mult), apart=False)
            link(eng.tensor_scalar(v[:, 2:3], st3[:, 1:2], LN_EPS, None, ALU.add), apart=False)
            link(eng.tensor_scalar(v[:, 3:5], ss[:, :], 1e-30, None, ALU.max))
            link(eng.tensor_tensor(msq[:, :], sq, msq[:, :], ALU.subtract))
            link(eng.tensor_scalar(v[:, 0:2], msq[:, :], 0.0, GN_EPS * GN_SCALE ** 2, ALU.max, ALU.add))
            link(eng.tensor_scalar(vm[:, :], v[:, :], -0.5, None, ALU.mult), apart=False)
            link(eng.tensor_scalar(y[:, :].bitcast(I32), v[:, :].bitcast(I32), -0.5, RSQRT_MAGIC,
                                    ALU.mult, ALU.add))
            for n in range(3):
                link(eng.tensor_tensor(t[:, :], y[:, :], y[:, :], ALU.mult))
                link(eng.tensor_tensor(t[:, :], t[:, :], vm[:, :], ALU.mult))
                link(eng.tensor_scalar(t[:, :], t[:, :], 1.5, None, ALU.add))
                link(eng.tensor_tensor(y[:, :], y[:, :], t[:, :], ALU.mult))
                if n in between:
                    between[n]()
            waits = ((gelu1_done, reached(i - GELU1, B)), (gelu2_done, reached((i - GELU2) * 2, 2 * B)),
                     (hid_done, reached(i - HID, B)), (rinv_done, reached(i - NORM, B)))
            wait_all(eng, passed, waits)
            scale, bias = c12[:, 0:4:2], c12[:, 1:4:2]
            link(eng.tensor_tensor(scale, y[:, 0:2], params[:, GN1:GN1 + 4:2], ALU.mult), apart=False)
            link(eng.tensor_tensor(c3[:, 1:2], st3[:, 0:1], y[:, 2:3], ALU.mult))
            link(eng.tensor_tensor(msq[:, :], mean, scale, ALU.mult))
            link(eng.tensor_tensor(bias, params[:, GN1 + 1:GN1 + 4:2], msq[:, :], ALU.subtract),
                 apart=False)
            assert link.n == GN_STEPS
            link(eng.tensor_scalar(c3[:, 1:2], c3[:, 1:2], -1.0, None, ALU.mult), apart=False)
            link(eng.tensor_scalar(c3[:, 0:1], y[:, 2:3], 1.0, None, ALU.mult), apart=False)
            assert link.n == LN_STEPS
            link(eng.tensor_tensor(nrm[:, :], v[:, 3:5], y[:, 3:5], ALU.mult))
            link(eng.tensor_scalar(nrm[:, :], nrm[:, :], RMS_EPS, None, ALU.add))
            link(eng.tensor_scalar(nrm[:, :], nrm[:, :], LN_S * AW_S, None, ALU.mult))
            assert link.n == NORM_STEPS

        @block.sync
        def _(sp):
            def load(b):
                sp.dma_start(x_f[0:CI, PAD:PAD + T], x_d[bass.ds(b, 1), :, :].rearrange("a c t -> (a c) t")
                             ).then_inc(x_loaded, 16)
                sp.dma_start(x_f[CI:P, PAD - 1:PAD - 1 + T],
                             x_d[bass.ds(b, 1), :, :].rearrange("a c t -> (a c) t")).then_inc(x_loaded, 16)

            sp.dma_start(raw["wc"], wc_d).then_inc(w_loaded["wc"], 16)
            sp.wait_ge(zeroed_x, 2)
            load(0)
            sp.dma_start(keep["params"][:, :], params_d).then_inc(w_loaded["params"], 16)
            sp.dma_start(raw["pw"], pw_d).then_inc(w_loaded["pw"], 16)
            sp.dma_start(raw["wqk"], wqk_d).then_inc(w_loaded["wqk"], 16)
            sp.dma_start(keep["consts"][:, :], consts_d).then_inc(w_loaded["consts"], 16)
            sp.dma_start(keep["gains"][:, :], rows_d.partition_broadcast(P)).then_inc(w_loaded["gains"], 16)
            with sp.Fori(1, B) as b:
                sp.wait_ge(x_hi, b)
                sp.wait_ge(x_lo, b)
                load(b)
            sp.wait_ge(x_hi, B)
            sp.wait_ge(x_lo, B)
            sp.dma_start(keep["wide0"][:, 0:RAW], heads_d[0, :, :]).then_inc(raw_loaded[0], 16)
            sp.wait_ge(conv_done, 4 * B)
            sp.dma_start(keep["wide1"][:, 0:RAW], heads_d[1, :, :]).then_inc(raw_loaded[1], 16)

        @block.scalar
        def _(act):
            scales = {"wc": CW_S, "pw": PW_S, "wqk": AW_S}

            def weights_high(n, at=slice(None)):
                act.wait_ge(w_loaded[n], 16)
                act.activation(keep[f"{n}_h"][:, at], raw[n][:, at], ACT.Copy, scale=scales[n]
                               ).then_inc(w_hi[n], 1)

            def copy_y1(i, p, c):
                act.wait_ge(conv_done, i * 4 + (c + 1))
                if c == 0:
                    need(act, gelu1_done, i - 1, B)
                act.activation(y1[p][:, c * CHUNK:(c + 1) * CHUNK], conv_ps[c % 2][:, :], ACT.Copy
                               ).then_inc(y1_copied, 1)
                if isinstance(i, int) and i == 1:
                    weights_high("wqk", QUARTERS[c])

            def hidden_high(b, hf):
                act.wait_ge(ht_done, b * 2 + (hf + 1))
                if hf == 0:
                    need(act, proj_done, b, B)
                act.activation(ht_h[:, hf * CHUNK:(hf + 1) * CHUNK], turn_ps[:, :], ACT.Copy,
                               scale=LN_S).then_inc(ht_hi, 1)

            def body(i, p, ok):
                if ok(0):
                    copy_y1(i, p, 0)
                if ok(PROJ):
                    hidden_high(i - PROJ, 0)
                if ok(-1):
                    act.wait_ge(x_loaded, i * 32 + 64)
                    need(act, conv_done, i * 4, 4 * B)
                    act.activation(x_h[1 - p][:, :], x_f[:, :], ACT.Copy).then_inc(x_hi, 1)
                if isinstance(i, int) and i == 0:
                    weights_high("pw")
                if isinstance(i, int) and i == 2:
                    act.wait_ge(w_loaded["consts"], 16)
                    act.activation(keep["ident_h"][:, :], ident, ACT.Copy).then_inc(ident_done, 1)
                if ok(0):
                    copy_y1(i, p, 1)
                if ok(PROJ):
                    hidden_high(i - PROJ, 1)
                if ok(0):
                    copy_y1(i, p, 2)
                if ok(0):
                    copy_y1(i, p, 3)
                if ok(DW):
                    b = i - DW
                    act.wait_ge(dw_step, b * DW_TAPS + DW_TAPS)
                    need(act, pw_done, b * 2, 2 * B)
                    act.activation(dw_h[:, :], dw[:, :], ACT.Copy, scale=DW_S).then_inc(dw_hi, 1)
                if ok(GELU2):
                    b = i - GELU2
                    act.wait_ge(norm_step, (i - 1) * NORM_STEPS + GN_STEPS)
                    for hf in range(2):
                        act.activation(resid[:, bass.ds(b * D + hf * CHUNK, CHUNK)], pw_ps[hf][:, :],
                                       ACT.Gelu, bias=c12[:, 3:4], scale=c12[:, 2:3]).then_inc(gelu2_done, 1)
                if ok(GELU1):
                    act.wait_ge(norm_step, (i - 1) * NORM_STEPS + GN_STEPS)
                    need(act, dw_step, (i - DW + 1) * DW_TAPS, B * DW_TAPS)
                    act.activation(g1[:, DW_PAD:DW_PAD + T], y1[1 - p][:, :], ACT.Gelu, bias=c12[:, 1:2],
                                   scale=c12[:, 0:1]).then_inc(gelu1_done, 1)
                if ok(NORM):
                    b = i - NORM
                    act.wait_ge(tail1_done, b + 1)
                    act.activation(keep["qct_h"][:, :, bass.ds(b * P, P)],
                                   turn_ps[:, 0:QR].rearrange("p (k n) -> p k n", k=QT),
                                   ACT.Copy, scale=QC_S).then_inc(t1_hi, 1)
                    act.activation(keep["kct_h"][:, bass.ds(b * P, P)], turn_ps[:, QR:QR + P],
                                   ACT.Copy, scale=KC_S).then_inc(t1_hi, 1)
                    act.activation(keep["kc_h"][:, bass.ds(b * P, P)], k_n[:, :], ACT.Copy, scale=KC_S
                                   ).then_inc(kc_hi, 1)
                if ok(HID):
                    b = i - HID
                    act.wait_ge(norm_step, (i - 1) * NORM_STEPS + LN_STEPS)
                    need(act, ht_done, b * 2, 2 * B)
                    act.activation(hid[:, :], resid[:, bass.ds(b * D, D)], ACT.Identity, bias=c3[:, 1:2],
                                   scale=c3[:, 0:1]).then_inc(hid_done, 1)
                if ok(PROJ):
                    b = i - PROJ
                    act.wait_ge(proj_done, b + 1)
                    need(act, norm_step, i * NORM_STEPS, (LAST + NORM) * NORM_STEPS)
                    need(act, ss_done, b * 2, 2 * B)
                    act.activation(junk[:, :], q_ps[:, 0:QR], ACT.Square, scale=UN * QR ** -0.5,
                                   accum_out=ss[:, 0:1]).then_inc(ss_done, 1)
                    act.wait_ge(ss_done, b * 2 + 1)
                    act.activation(junk[:, 0:KVR], kv_ps[:, 0:KVR], ACT.Square, scale=UN * KVR ** -0.5,
                                   accum_out=ss[:, 1:2]).then_inc(ss_done, 1)
                if ok(NORM):
                    b = i - NORM
                    act.wait_ge(tail2_done, b + 1)
                    act.activation(keep["kr_h"][:, bass.ds(b * P, P)], turn_ps[:, 0:P], ACT.Copy,
                                   scale=KR_S * UN).then_inc(t2_hi, 1)

            weights_high("wc")
            act.wait_ge(zeroed, 5)
            pipeline(act, body, -1, lags, NORM)

        @block.gpsimd
        def _(pool):
            pool.memset(g1[:, 0:DW_PAD], 0.0).then_inc(zeroed, 1)
            pool.memset(g1[:, DW_PAD + T:], 0.0).then_inc(zeroed, 1)
            pool.memset(st[:, :], 1.0).then_inc(zeroed, 1)
            pool.memset(st3[:, :], 1.0).then_inc(zeroed, 1)
            pool.memset(ss[:, :], 1.0).then_inc(zeroed, 1)

            def body(i, p, ok):
                if not isinstance(i, int) or 1 <= i <= LAST + DW:
                    norms(pool, i, pool_passed)
                if ok(-1) and (not isinstance(i, int) or i >= 0):
                    wait_apart(pool, pool_passed, (x_hi, i + 2))
                    pool.tensor_tensor(x_l[1 - p][:, :], x_f[:, :], x_h[1 - p][:, :], ALU.subtract
                                       ).then_inc(x_lo, 1)

            pool.memset(keep["mean_mat"][:, :], 1.0 / P).then_inc(zeroed, 1)
            pool.wait_ge(zeroed, 5)
            pool.wait_ge(w_loaded["params"], 16)
            pipeline(pool, body, -1, lags, NORM)

        @block.vector
        def _(dve):
            dve.memset(x_f[:, 0:PAD], 0.0).then_inc(zeroed_x, 1)
            dve.memset(x_f[:, PAD - 1 + T:], 0.0).then_inc(zeroed_x, 1)

            def low(out, src, scale, high, done):
                dve.scalar_tensor_tensor(out=out, in0=src, scalar=scale, in1=high, op0=ALU.mult,
                                         op1=ALU.subtract).then_inc(done, 1)

            def weights_low(n, scale, at=slice(None), part=0):
                dve.wait_ge(w_hi[n], part + 1)
                low(keep[f"{n}_l"][:, at], raw[n][:, at], scale, keep[f"{n}_h"][:, at], w_lo[n])

            def stats1(i, p, c):
                dve.wait_ge(y1_copied, i * 4 + (c + 1))
                dve.bn_stats(bn1[:, c, :], y1[p][:, c * CHUNK:(c + 1) * CHUNK]).then_inc(bn1_done, 1)
                if isinstance(i, int) and i == 1:
                    weights_low("wqk", AW_S, QUARTERS[c], c)

            def mean_and_square(ready, b, out, bn):
                link = Chain(dve, ready, b, 2)
                link(dve.bn_aggr(out, bn))
                link(dve.scalar_tensor_tensor(out=out[:, 1:2], in0=out[:, 0:1], scalar=out[:, 0:1],
                                              in1=out[:, 1:2], op0=ALU.mult, op1=ALU.add))

            def tap(b, k):
                if k == 0:
                    dve.wait_ge(gelu1_done, b + 1)
                    need(dve, dw_hi, b, B)
                    dve.tensor_scalar(dw[:, :], g1[:, 0:2 * D:2], params[:, 0:1], params[:, 5:6],
                                      ALU.mult, ALU.add).then_inc(dw_step, 1)
                else:
                    dve.wait_ge(dw_step, b * DW_TAPS + k)
                    dve.scalar_tensor_tensor(out=dw[:, :], in0=g1[:, k:k + 2 * D - 1:2],
                                             scalar=params[:, k:k + 1], in1=dw[:, :],
                                             op0=ALU.mult, op1=ALU.add).then_inc(dw_step, 1)

            def hidden_low(b, hf):
                dve.wait_ge(ht_hi, b * 2 + (hf + 1))
                sl = slice(hf * CHUNK, (hf + 1) * CHUNK)
                low(ht_l[:, sl], turn_ps[:, :], LN_S, ht_h[:, sl], ht_lo)

            def take_latents(b):
                dve.wait_ge(proj_done, b + 1)
                dve.wait_ge(ss_done, b * 2 + 2)
                need(dve, tail1_done, b, B)
                need(dve, kn_done, b, B)
                dve.tensor_tensor(q_g[:, :], q_ps[:, 0:QR], gains[:, 0:QR], ALU.mult).then_inc(q_taken, 1)
                dve.tensor_tensor(k_g[:, :], kv_ps[:, 0:KVR], gains[:, QR:QR + KVR], ALU.mult
                                  ).then_inc(q_taken, 1)
                HR = RD // 2
                need(dve, kr_step, b * 5, 5 * B)
                dve.tensor_tensor(kr_a[:, :], kv_ps[:, KVR:KVR + RD], cos, ALU.mult).then_inc(kr_step, 1)
                dve.tensor_tensor(kr_b[:, 0:HR], kv_ps[:, KVR + HR:KVR + RD], sin[:, 0:HR], ALU.mult
                                  ).then_inc(kr_step, 1)
                dve.tensor_tensor(kr_b[:, HR:RD], kv_ps[:, KVR:KVR + HR], sin[:, HR:RD], ALU.mult
                                  ).then_inc(kr_step, 1)

            def add_rotary(b):
                dve.wait_ge(kr_step, b * 5 + 3)
                need(dve, tail2_done, b, B)
                for half in range(2):
                    dve.tensor_tensor(kr2[:, half * RD:(half + 1) * RD], kr_a[:, :], kr_b[:, :], ALU.add
                                      ).then_inc(kr_step, 1)

            def latent_norms(i, b):
                dve.wait_ge(norm_step, i * NORM_STEPS)
                need(dve, kn_done, b, B)
                dve.reciprocal(rinv[:, :], nrm[:, :]).then_inc(rinv_done, 1)
                dve.wait_ge(rinv_done, b + 1)
                dve.wait_ge(q_taken, b * 2 + 2)
                need(dve, tail1_done, b, B)
                need(dve, kc_lo, b, B)
                dve.tensor_scalar(diag[:, :], ident, rinv[:, 0:1], None, ALU.mult).then_inc(diag_done, 1)
                dve.tensor_scalar(k_n[:, :], k_g[:, :], rinv[:, 1:2], None, ALU.mult).then_inc(kn_done, 1)

            def body(i, p, ok):
                if isinstance(i, int) and i == -1:
                    dve.wait_ge(x_hi, 1)
                    dve.tensor_tensor(x_l[1 - p][:, :], x_f[:, :], x_h[1 - p][:, :], ALU.subtract
                                      ).then_inc(x_lo, 1)
                if isinstance(i, int) and i == 0:
                    weights_low("pw", PW_S)
                if isinstance(i, int) and i == 2:
                    for n in ("consts", "gains"):
                        dve.wait_ge(w_loaded[n], 16)
                if ok(GELU1) or ok(GELU2):
                    dve.wait_ge(stat_done, i)
                    need(dve, norm_step, (i - 1) * NORM_STEPS, (LAST + NORM) * NORM_STEPS)
                    dve.tensor_copy(s[:, :], stat_ps[:, 0:4]).then_inc(s_copied, 1)
                late = isinstance(i, int) and i > LAST + DW
                if late:
                    lows = {hf: lambda hf=hf: hidden_low(i - PROJ, hf) for hf in range(2)} if ok(PROJ) else {}
                    norms(dve, i, between=lows)
                if ok(DW):
                    tap(i - DW, 0)
                if ok(PROJ) and not late:
                    hidden_low(i - PROJ, 0)
                if ok(DW):
                    tap(i - DW, 1)
                if ok(0):
                    stats1(i, p, 0)
                if ok(DW):
                    tap(i - DW, 2)
                if ok(PROJ) and not late:
                    hidden_low(i - PROJ, 1)
                if ok(DW):
                    tap(i - DW, 3)
                if ok(0):
                    stats1(i, p, 1)
                if ok(DW):
                    tap(i - DW, 4)
                if ok(0):
                    stats1(i, p, 2)
                if ok(NORM):
                    latent_norms(i, i - NORM)
                if ok(DW):
                    b = i - DW
                    dve.wait_ge(dw_hi, b + 1)
                    need(dve, pw_done, b * 2, 2 * B)
                    low(dw_l[:, :], dw[:, :], DW_S, dw_h[:, :], dw_lo)
                if ok(0):
                    stats1(i, p, 3)
                    waits = [(bn1_done, i * 4 + 4)]
                    if not isinstance(i, int) or i >= 1:
                        waits.append((stat_done, i))
                    wait_apart(dve, dve_passed, *waits)
                    mean_and_square(st1_ready, i, st[:, 0:2], bn1[:, :, :])
                if ok(GELU2):
                    b = i - GELU2
                    dve.wait_ge(gelu2_done, b * 2 + 2)
                    for hf in range(2):
                        dve.bn_stats(bn3[:, hf, :], resid[:, bass.ds(b * D + hf * CHUNK, CHUNK)]
                                     ).then_inc(ln_step, 1)
                    wait_apart(dve, dve_passed, (ln_step, b * 3 + 2), (norm_step, i * NORM_STEPS))
                    dve.bn_aggr(st3[:, :], bn3[:, :, :]).then_inc(ln_step, 1)
                if ok(NORM):
                    b = i - NORM
                    dve.wait_ge(t1_hi, b * 2 + 2)
                    low(keep["qct_l"][:, :, bass.ds(b * P, P)],
                        turn_ps[:, 0:QR].rearrange("p (k n) -> p k n", k=QT), QC_S,
                        keep["qct_h"][:, :, bass.ds(b * P, P)], t1_lo)
                    low(keep["kct_l"][:, bass.ds(b * P, P)], turn_ps[:, QR:QR + P], KC_S,
                        keep["kct_h"][:, bass.ds(b * P, P)], t1_lo)
                    dve.wait_ge(kc_hi, b + 1)
                    low(keep["kc_l"][:, bass.ds(b * P, P)], k_n[:, :], KC_S,
                        keep["kc_h"][:, bass.ds(b * P, P)], kc_lo)
                if ok(DW):
                    b = i - DW
                    for hf in range(2):
                        dve.wait_ge(pw_done, b * 2 + (hf + 1))
                        dve.bn_stats(bn2[:, hf, :], pw_ps[hf][:, :]).then_inc(bn2_done, 1)
                    wait_apart(dve, dve_passed, (bn2_done, b * 2 + 2), (stat_done, i))
                    mean_and_square(st2_ready, b, st[:, 2:4], bn2[:, :, :])
                if ok(PROJ):
                    take_latents(i - PROJ)
                if ok(NORM):
                    b = i - NORM
                    dve.wait_ge(t2_hi, b + 1)
                    low(keep["kr_l"][:, bass.ds(b * P, P)], turn_ps[:, 0:P], KR_S * UN,
                        keep["kr_h"][:, bass.ds(b * P, P)], t2_lo)
                if ok(PROJ):
                    add_rotary(i - PROJ)

            weights_low("wc", CW_S)
            dve.wait_ge(zeroed, 5)
            dve.wait_ge(w_loaded["params"], 16)
            pipeline(dve, body, -1, lags, NORM)

        @block.tensor
        def _(pe):
            def conv(i, p, c):
                if c == 0:
                    pe.wait_ge(x_lo, i + 1)
                need(pe, y1_copied, i * 4 + (c - 1), 4 * B)
                n = 0
                for w, x in ((wc_h, x_h), (wc_l, x_h), (wc_h, x_l)):
                    for m in range(PAIRS):
                        lo = c * CHUNK + 2 * m
                        last = pe.matmul(conv_ps[c % 2][:, :], w[:, m, :], x[p][:, lo:lo + CHUNK],
                                         start=n == 0, stop=n == 3 * PAIRS - 1)
                        n += 1
                last.then_inc(conv_done, 1)

            def turn_hidden(i, hf):
                b = i - PROJ
                if hf == 0:
                    pe.wait_ge(hid_done, b + 1)
                    need(pe, t2_lo, i - NORM, B)
                need(pe, ht_lo, b * 2 + hf, 2 * B)
                for k in range(4):
                    last = pe.transpose(turn_ps[:, k * P:(k + 1) * P],
                                        hid[:, (4 * hf + k) * P:(4 * hf + k + 1) * P], ident)
                last.then_inc(ht_done, 1)

            def pointwise(i):
                b = i - DW
                pe.wait_ge(dw_lo, b + 1)
                need(pe, gelu2_done, b * 2, 2 * B)
                for hf in range(2):
                    sl = slice(hf * CHUNK, (hf + 1) * CHUNK)
                    pe.matmul(pw_ps[hf][:, :], keep["pw_h"][:, :], dw_h[:, sl], start=True, stop=False)
                    pe.matmul(pw_ps[hf][:, :], keep["pw_l"][:, :], dw_h[:, sl], start=False, stop=False)
                    pe.matmul(pw_ps[hf][:, :], keep["pw_h"][:, :], dw_l[:, sl], start=False, stop=True
                              ).then_inc(pw_done, 1)

            def project(i, hf):
                b = i - PROJ
                if hf == 0:
                    need(pe, q_taken, b * 2, 2 * B)
                    need(pe, kr_step, b * 5 - 2, 5 * B)
                pe.wait_ge(ht_lo, b * 2 + (hf + 1))
                for k in range(hf * (KT // 2), (hf + 1) * (KT // 2)):
                    for n, (h, w) in enumerate(((ht_h, wqk_h), (ht_h, wqk_l), (ht_l, wqk_h))):
                        lhs = h[:, k * P:(k + 1) * P]
                        first, end = k == 0 and n == 0, k == KT - 1 and n == 2
                        pe.matmul(q_ps[:, 0:QR], lhs, w[:, k, 0:QR], start=first, stop=end)
                        last = pe.matmul(kv_ps[:, 0:KVR + RD], lhs, w[:, k, QR:QR + KVR + RD],
                                         start=first, stop=end)
                if hf:
                    last.then_inc(proj_done, 1)

            def body(i, p, ok):
                if isinstance(i, int) and i == 1:
                    pe.wait_ge(zeroed, 6)
                if isinstance(i, int) and i == 2:
                    pe.wait_ge(w_lo["pw"], 1)
                if isinstance(i, int) and i == 3:
                    pe.wait_ge(w_lo["wqk"], 4)
                    pe.wait_ge(w_loaded["consts"], 16)
                if ok(0):
                    conv(i, p, 0)
                if ok(GELU1) or ok(GELU2):
                    need(pe, st1_ready, i * 2, 2 * B)
                    need(pe, st2_ready, (i - GELU2) * 2 + 2, 2 * B)
                    need(pe, s_copied, i - 1, LAST + GELU2)
                    pe.matmul(stat_ps[:, 0:4], keep["mean_mat"][:, :], st[:, :], start=True, stop=True
                              ).then_inc(stat_done, 1)
                if ok(PROJ):
                    turn_hidden(i, 0)
                if ok(0):
                    conv(i, p, 1)
                if ok(PROJ):
                    turn_hidden(i, 1)
                if ok(0):
                    conv(i, p, 2)
                if ok(0):
                    conv(i, p, 3)
                if ok(PROJ):
                    project(i, 0)
                if ok(NORM):
                    b = i - NORM
                    pe.wait_ge(diag_done, b + 1)
                    pe.wait_ge(kn_done, b + 1)
                    need(pe, ht_lo, b * 2 + 4, 2 * B)
                    for k in range(QT):
                        pe.matmul(turn_ps[:, k * P:(k + 1) * P], q_g[:, k * P:(k + 1) * P], diag[:, :],
                                  start=True, stop=True)
                    pe.transpose(turn_ps[:, QR:QR + P], k_n[:, :], ident).then_inc(tail1_done, 1)
                if ok(DW):
                    pointwise(i)
                if ok(PROJ):
                    project(i, 1)
                if ok(NORM):
                    b = i - NORM
                    pe.wait_ge(kr_step, b * 5 + 5)
                    pe.wait_ge(t1_lo, b * 2 + 2)
                    pe.transpose(turn_ps[:, 0:P], kr2[:, :], ident).then_inc(tail2_done, 1)

            pe.wait_ge(w_lo["wc"], 1)
            pipeline(pe, body, 0, lags, NORM)


def fresh(eng, value, most):
    if isinstance(value, int):
        return value
    register = eng.alloc_register(None)
    eng.reg_mov(register, value)
    return eng.snap(register, min_val=0, max_val=most)


class Round:

    def __init__(self, eng, t, parity=None):
        self.eng, self.t, self.known, self.kept = eng, t, isinstance(t, int), {}
        self.parity = t % 2 if self.known else parity

    def held(self, name, value, most):
        if name not in self.kept:
            self.kept[name] = fresh(self.eng, value, most)
        return self.kept[name]

    @property
    def slot(self):
        return self.held("slot", self.t * QUAD, ROUNDS * QUAD)

    @property
    def group(self):
        return self.held("group", self.t // QUADS, GROUPS)

    @property
    def side(self):
        return self.held("side", (self.t // QUADS) % 2, 1)

    @property
    def tok(self):
        return self.held("tok", (self.t % QUADS) * (QUAD * P), TOK - QUAD * P)

    @property
    def half(self):
        if self.parity is not None:
            return self.parity * (HEADS * CHUNK)
        return self.held("half", (self.t % 2) * (HEADS * CHUNK), HEADS * CHUNK)

    @property
    def place(self):
        return self.held("place", self.t % HEADS, HEADS - 1)


def attention_phase(nc, keep, raw_loaded, heads_d):
    with ExitStack() as ctx:
        def sb(name, shape, dt=F32):
            return ctx.enter_context(nc.sbuf_tensor(name, shape, dt))

        def pb(name, dt=F32):
            return ctx.enter_context(nc.psum_tensor(name, [P, CHUNK], dt))

        def sem(name):
            return ctx.enter_context(nc.semaphore(name))

        raws = [keep["wide0"], keep["wide1"]]
        wp_h, wp_l = sb("wp_h", [P, 2, QT, HEADS, P], F16), sb("wp_l", [P, 2, QT, HEADS, P], F16)
        wr_h, wr_l = sb("wr_h", [P, 2, QT, HEADS * RD], F16), sb("wr_l", [P, 2, QT, HEADS * RD], F16)
        m_h, m_l = sb("m_h", [P, 2 * HEADS * D], F16), sb("m_l", [P, 2 * HEADS * D], F16)
        qp_h, qp_l = sb("qp_h", [P, 2 * HEADS * CHUNK], F16), sb("qp_l", [P, 2 * HEADS * CHUNK], F16)
        ra, rb, rz = (sb(n, [P, HEADS, RD]) for n in ("ra", "rb", "rz"))
        z = sb("z", [P, HEADS, 2 * RD], F16)
        zt = sb("zt", [P, HEADS, P], F16)
        prob = sb("prob", [P, HEADS, P])
        pt_h, pt_l = sb("pt_h", [P, CHUNK], F16), sb("pt_l", [P, CHUNK], F16)
        ot_h, ot_l = sb("ot_h", [P, HEADS, P], F16), sb("ot_l", [P, HEADS, P], F16)
        mx, nmx, rsum, rrec = (sb(n, [P, HEADS]) for n in ("mx", "nmx", "rsum", "rrec"))
        qp_ps, prod_ps, rope_ps, zt_ps = pb("qp_ps"), pb("prod_ps"), pb("rope_ps"), pb("zt_ps", F16)
        s_ps, pt_ps, out_ps = pb("s_ps"), pb("pt_ps"), [pb("out_ps0"), pb("out_ps1")]
        start_banks = [prod_ps, s_ps, *out_ps]
        (prod_done, prod_hi, prod_lo, wr_hi, wr_lo, qp_done, qp_hi, qp_lo, rope_done, rot_step,
         z_hi, z_lo, zt_done, zt_copied, s_done, max_step, exp_done, norm_step, pt_done, pt_hi, pt_lo,
         av_done, o_hi, o_lo, out_done, out_added) = (sem(n) for n in (
             "prod_done prod_hi prod_lo wr_hi wr_lo qp_done qp_hi qp_lo rope_done rot_step "
             "z_hi z_lo zt_done zt_copied s_done max_step exp_done norm_step pt_done pt_hi pt_lo "
             "av_done o_hi o_lo out_done out_added").split())
        resid, ident, ident_h = keep["resid"], keep["consts"][:, 0:P], keep["ident_h"]
        cos, sin = keep["consts"][:, P:P + RD], keep["consts"][:, P + RD:P + 2 * RD]
        qct_h, qct_l, kct_h, kct_l = keep["qct_h"], keep["qct_l"], keep["kct_h"], keep["kct_l"]
        kc_h, kc_l, kr_h, kr_l = keep["kc_h"], keep["kc_l"], keep["kr_h"], keep["kr_l"]
        EXP_SCALE = QK ** -0.5 / (QP_S * KC_S)
        block = ctx.enter_context(nc.Block())

        def rounds(eng, start, body):
            def run(t, more, parity=None):
                def at(k):
                    if isinstance(t, int) and not 0 <= t + k < ROUNDS:
                        return None
                    return Round(eng, t + k if k else t, parity if k == 0 or parity is None else 1 - parity)

                body(at(-1), at(0), at(1), more)

            start()
            run(0, True)
            with eng.Fori(1, ROUNDS - HEADS - 2, 2) as t:
                run(t, True, 1)
                run(t + 1, True, 0)
            run(ROUNDS - HEADS - 1, True)
            with eng.Fori(ROUNDS - HEADS, ROUNDS - 1) as t:
                run(t, False)
            run(ROUNDS - 1, False)

        @block.sync
        def _(sp):
            def load(h, p):
                sp.dma_start(raws[p][:, 0:RAW], heads_d[bass.ds(h, 1), :, :].rearrange("a p n -> (a p) n")
                             ).then_inc(raw_loaded[p], 16)

            with sp.Fori(2, NH - 1, 2) as h:
                head = [h, fresh(sp, h + 1, NH - 1)]
                split = [fresh(sp, h - 1, NH), h]
                used = [fresh(sp, h * 3 - 3, 3 * NH), fresh(sp, h * 3, 3 * NH)]
                for p in range(2):
                    sp.wait_ge(prod_done, used[p])
                    sp.wait_ge(wr_lo, split[p])
                    load(head[p], p)

        @block.scalar
        def _(act):
            def high(out, src, scale, done):
                act.activation(out, src, ACT.Copy, scale=scale).then_inc(done, 1)

            def prod_high(h, p, sd, k, part, bank, fresh):
                act.wait_ge(prod_done, h * 3 + part + 1)
                if part == 0:
                    high(wp_h[:, bass.ds(sd, 1), :, bass.ds(k, 1), :].rearrange("p a t k n -> p (a t) (k n)"),
                         bank[:, 0:QR].rearrange("p (t n) -> p t n", t=QT), WP_S, prod_hi)
                    if not fresh:
                        act.wait_ge(rope_done, h * 4 - 15)
                    high(wr_h[:, bass.ds(sd, 1), :, bass.ds(k * RD, RD)].rearrange("p a t n -> p (a t) n"),
                         raws[p][:, RAW_R:RAW].rearrange("p (t n) -> p t n", t=QT), WR_S, wr_hi)
                else:
                    if not fresh:
                        act.wait_ge(out_done, h * 8 - 31)
                    high(m_h[:, bass.ds((sd * HEADS + k) * D + (part - 1) * CHUNK, CHUNK)], bank[:, :],
                         M_S, prod_hi)

            def query_high(r, j, bank=qp_ps):
                act.wait_ge(qp_done, r.slot + (j + 1))
                if not r.known or r.t >= 2:
                    act.wait_ge(s_done, r.slot - 4)
                high(qp_h[:, bass.ds(r.half + j * CHUNK, CHUNK)], bank[:, :],
                     QP_S / (QC_S * WP_S), qp_hi)

            def rope_high(s):
                act.wait_ge(rot_step, s * 4 + 4)
                if not isinstance(s, int) or s >= 1:
                    act.wait_ge(zt_done, s)
                high(z[:, :, 0:RD], rz[:, :, :], QRO_S / (QC_S * WR_S), z_hi)

            def rope_copy(s):
                act.wait_ge(zt_done, s + 1)
                if not isinstance(s, int) or s >= 1:
                    act.wait_ge(s_done, s)
                act.activation(zt[:, :, :].rearrange("p h n -> p (h n)"), zt_ps[:, :], ACT.Copy
                               ).then_inc(zt_copied, 1)

            def start():
                for h in range(HEADS):
                    for part in range(3):
                        prod_high(h, h % 2, 0, h, part, start_banks[(3 * h + part) % 4], True)
                    query_high(Round(act, 0), h, (qp_ps, pt_ps)[h % 2])
                rope_high(0)
                rope_copy(0)

            def body(before, now, after, more):
                for j in range(QUAD):
                    s = now.slot + j
                    act.wait_ge(max_step, s * 2 + 2)
                    if before or j:
                        act.wait_ge(pt_done, s)
                    for h in range(HEADS):
                        act.activation(prob[:, h, :], s_ps[:, h * P:(h + 1) * P], ACT.Exp,
                                       bias=nmx[:, h:h + 1], scale=EXP_SCALE,
                                       accum_out=rsum[:, h:h + 1]).then_inc(exp_done, 1)
                    if after or j < QUAD - 1:
                        rope_high(s + 1)
                    act.wait_ge(pt_done, s + 1)
                    if before or j:
                        act.wait_ge(av_done, s)
                    high(pt_h[:, :], pt_ps[:, :], PR_S, pt_hi)
                    if after:
                        query_high(after, j)
                    if after or j < QUAD - 1:
                        rope_copy(s + 1)
                    act.wait_ge(av_done, s + 1)
                    if before or j:
                        act.wait_ge(out_done, s * 2)
                    high(ot_h[:, :, :].rearrange("p h n -> p (h n)"), pt_ps[:, :], O_S / (PR_S * KC_S), o_hi)
                    if more and j:
                        prod_high(now.t + HEADS, now.parity, now.side * -1 + 1, now.place, j - 1, prod_ps, False)

            rounds(act, start, body)

        @block.vector
        def _(dve):
            def low(out, src, scale, high, done):
                dve.scalar_tensor_tensor(out=out, in0=src, scalar=scale, in1=high, op0=ALU.mult,
                                         op1=ALU.subtract).then_inc(done, 1)

            def prod_low(h, p, sd, k, part, bank):
                dve.wait_ge(prod_hi, h * 3 + part + 1)
                if part == 0:
                    at = (slice(None), bass.ds(sd, 1), slice(None), bass.ds(k, 1), slice(None))
                    low(wp_l[at].rearrange("p a t k n -> p (a t) (k n)"),
                        bank[:, 0:QR].rearrange("p (t n) -> p t n", t=QT), WP_S,
                        wp_h[at].rearrange("p a t k n -> p (a t) (k n)"), prod_lo)
                    dve.wait_ge(wr_hi, h + 1)
                    at = (slice(None), bass.ds(sd, 1), slice(None), bass.ds(k * RD, RD))
                    low(wr_l[at].rearrange("p a t n -> p (a t) n"),
                        raws[p][:, RAW_R:RAW].rearrange("p (t n) -> p t n", t=QT), WR_S,
                        wr_h[at].rearrange("p a t n -> p (a t) n"), wr_lo)
                else:
                    at = bass.ds((sd * HEADS + k) * D + (part - 1) * CHUNK, CHUNK)
                    low(m_l[:, at], bank[:, :], M_S, m_h[:, at], prod_lo)

            def query_low(r, j, bank=qp_ps):
                dve.wait_ge(qp_hi, r.slot + (j + 1))
                at = bass.ds(r.half + j * CHUNK, CHUNK)
                low(qp_l[:, at], bank[:, :], QP_S / (QC_S * WP_S), qp_h[:, at], qp_lo)

            HR = RD // 2

            def rotate(s):
                dve.wait_ge(rope_done, s + 1)
                x = rope_ps[:, 0:HEADS * RD].rearrange("p (h n) -> p h n", h=HEADS)
                dve.tensor_tensor(ra[:, :, :], x, cos[:, None, :].broadcast_to([P, HEADS, RD]), ALU.mult
                                  ).then_inc(rot_step, 1)
                dve.tensor_tensor(rb[:, :, 0:HR], x[:, :, HR:RD],
                                  sin[:, None, 0:HR].broadcast_to([P, HEADS, HR]), ALU.mult
                                  ).then_inc(rot_step, 1)
                dve.tensor_tensor(rb[:, :, HR:RD], x[:, :, 0:HR],
                                  sin[:, None, HR:RD].broadcast_to([P, HEADS, HR]), ALU.mult
                                  ).then_inc(rot_step, 1)
                dve.wait_ge(rot_step, s * 4 + 3)
                if not isinstance(s, int) or s >= 1:
                    dve.wait_ge(z_hi, s)
                dve.tensor_tensor(rz[:, :, :], ra[:, :, :], rb[:, :, :], ALU.add).then_inc(rot_step, 1)

            def rope_low(s):
                dve.wait_ge(z_hi, s + 1)
                low(z[:, :, RD:2 * RD], rz[:, :, :], QRO_S / (QC_S * WR_S), z[:, :, 0:RD], z_lo)

            def add_out(r, j, hf):
                dve.wait_ge(out_done, r.slot * 2 + (j * 2 + hf + 1))
                at = bass.ds(r.tok * (D // P) + (j * D + hf * CHUNK), CHUNK)
                dve.scalar_tensor_tensor(out=resid[:, at], in0=out_ps[hf][:, :], scalar=1.0 / (O_S * M_S),
                                         in1=resid[:, at], op0=ALU.mult, op1=ALU.add).then_inc(out_added, 1)

            def start():
                for h in range(HEADS):
                    for part in range(3):
                        prod_low(h, h % 2, 0, h, part, start_banks[(3 * h + part) % 4])
                    query_low(Round(dve, 0), h, (qp_ps, pt_ps)[h % 2])
                rotate(0)
                rope_low(0)

            def body(before, now, after, more):
                for j in range(QUAD):
                    s = now.slot + j
                    dve.wait_ge(s_done, s + 1)
                    dve.tensor_reduce(mx[:, :], s_ps[:, :].rearrange("p (h n) -> p h n", h=HEADS), AX.X,
                                      ALU.max).then_inc(max_step, 1)
                    dve.wait_ge(max_step, s * 2 + 1)
                    if before or j:
                        dve.wait_ge(exp_done, s * 4)
                    dve.tensor_scalar(nmx[:, :], mx[:, :], -EXP_SCALE, None, ALU.mult).then_inc(max_step, 1)
                    if after or j < QUAD - 1:
                        rotate(s + 1)
                    dve.wait_ge(exp_done, s * 4 + 4)
                    dve.reciprocal(rrec[:, :], rsum[:, :]).then_inc(norm_step, 1)
                    dve.wait_ge(norm_step, s * 2 + 1)
                    dve.tensor_tensor(prob[:, :, :], prob[:, :, :],
                                      rrec[:, :, None].broadcast_to([P, HEADS, P]), ALU.mult
                                      ).then_inc(norm_step, 1)
                    behind = (now, j - 1) if j else (before, QUAD - 1)
                    if behind[0]:
                        add_out(*behind, 0)
                    if after or j < QUAD - 1:
                        rope_low(s + 1)
                    if behind[0]:
                        add_out(*behind, 1)
                    dve.wait_ge(pt_hi, s + 1)
                    low(pt_l[:, :], pt_ps[:, :], PR_S, pt_h[:, :], pt_lo)
                    if after:
                        query_low(after, j)
                    dve.wait_ge(o_hi, s + 1)
                    low(ot_l[:, :, :].rearrange("p h n -> p (h n)"), pt_ps[:, :], O_S / (PR_S * KC_S),
                        ot_h[:, :, :].rearrange("p h n -> p (h n)"), o_lo)
                    if more and j:
                        prod_low(now.t + HEADS, now.parity, now.side * -1 + 1, now.place, j - 1, prod_ps)
                if not after:
                    for hf in range(2):
                        add_out(now, QUAD - 1, hf)
                    dve.wait_ge(out_added, ROUNDS * 8)

            rounds(dve, start, body)

        @block.tensor
        def _(pe):
            def products(h, p, part, bank, free):
                raw = raws[p]
                if part == 0:
                    pe.wait_ge(raw_loaded[p], (h - p) * 8 + 16)
                if not isinstance(free, int) or free > 0:
                    pe.wait_ge(prod_lo, free)
                if part == 0:
                    for k in range(QT):
                        last = pe.matmul(bank[:, k * P:(k + 1) * P], raw[:, RAW_Q + k * P:RAW_Q + (k + 1) * P],
                                         raw[:, RAW_K:RAW_K + P], start=True, stop=True)
                else:
                    at = RAW_O + (part - 1) * CHUNK
                    last = pe.matmul(bank[:, :], raw[:, RAW_V:RAW_V + P], raw[:, at:at + CHUNK],
                                     start=True, stop=True)
                last.then_inc(prod_done, 1)

            def queries(r, j, bank=qp_ps, free=0):
                pe.wait_ge(prod_lo, r.group * (3 * HEADS) + (3 * j + 1))
                if not r.known or r.t or j > free:
                    pe.wait_ge(qp_lo, r.slot + (j - free))
                side, tok = fresh(pe, r.side, 1), fresh(pe, r.tok, TOK - QUAD * P)
                n = 0
                for w, q in ((wp_h, qct_h), (wp_l, qct_h), (wp_h, qct_l)):
                    for k in range(QT):
                        last = pe.matmul(bank[:, :],
                                         w[:, bass.ds(side, 1), k, j, :].rearrange("p a n -> p (a n)"),
                                         q[:, k, bass.ds(tok, CHUNK)], start=n == 0, stop=n == 3 * QT - 1)
                        n += 1
                last.then_inc(qp_done, 1)

            def rope(r, j):
                if j == 0:
                    pe.wait_ge(wr_lo, r.group * HEADS + HEADS)
                if not r.known or r.t or j:
                    pe.wait_ge(rot_step, r.slot * 4 + (4 * j - 1))
                side, tok = fresh(pe, r.side, 1), fresh(pe, r.tok, TOK - QUAD * P)
                n = 0
                for q, w in ((qct_h, wr_h), (qct_h, wr_l), (qct_l, wr_h)):
                    for k in range(QT):
                        last = pe.matmul(rope_ps[:, 0:HEADS * RD], q[:, k, bass.ds(tok + j * P, P)],
                                         w[:, bass.ds(side, 1), k, :].rearrange("p a n -> p (a n)"),
                                         start=n == 0, stop=n == 3 * QT - 1)
                        n += 1
                last.then_inc(rope_done, 1)

            def turn_rope(s):
                pe.wait_ge(z_lo, s + 1)
                if not isinstance(s, int) or s >= 1:
                    pe.wait_ge(zt_copied, s)
                for h in range(HEADS):
                    last = pe.transpose(zt_ps[:, h * P:(h + 1) * P], z[:, h, :], ident_h[:, :])
                last.then_inc(zt_done, 1)

            def score_operands(r, j):
                keys = bass.ds(fresh(pe, r.tok, TOK - QUAD * P) + j * P, P)
                half = fresh(pe, r.half, HEADS * CHUNK)
                q = [bass.ds(half + (j * P + h * CHUNK), P) for h in range(HEADS)]
                operands = ([qp_h[:, at] for at in q], [qp_l[:, at] for at in q],
                            kct_h[:, keys], kct_l[:, keys], kr_h[:, keys], kr_l[:, keys])
                for ap in (*operands[2:], *operands[0], *operands[1]):
                    if not r.known:
                        pe.lower_ap(ap)
                return operands

            def scores(r, j, operands):
                q_h, q_l, k_h, k_l, rope_h, rope_l = operands
                if j == 0:
                    pe.wait_ge(qp_lo, r.slot + 4)
                if not r.known or r.t or j:
                    pe.wait_ge(exp_done, r.slot * 4 + 4 * j)
                out = [s_ps[:, h * P:(h + 1) * P] for h in range(HEADS)]
                for h in range(HEADS):
                    pe.matmul(out[h], q_h[h], k_h, start=h == 0, stop=False)
                    pe.matmul(out[h], q_h[h], k_l, start=False, stop=False)
                    pe.matmul(out[h], q_l[h], k_h, start=False, stop=False)
                pe.wait_ge(zt_copied, r.slot + (j + 1))
                for h in range(HEADS):
                    pe.matmul(out[h], zt[:, h, :], rope_h, start=False, stop=False)
                    last = pe.matmul(out[h], zt[:, h, :], rope_l, start=False, stop=h == HEADS - 1)
                last.then_inc(s_done, 1)

            def outputs(r, j):
                pe.wait_ge(o_lo, r.slot + (j + 1))
                if j == 0:
                    pe.wait_ge(prod_lo, r.group * (3 * HEADS) + 3 * HEADS)
                side = fresh(pe, r.side, 1)
                for hf in range(2):
                    if not r.known or r.t or j:
                        pe.wait_ge(out_added, r.slot * 2 + (j * 2 + hf - 1))
                    for h in range(HEADS):
                        at = bass.ds(side * (HEADS * D) + (h * D + hf * CHUNK), CHUNK)
                        pe.matmul(out_ps[hf][:, :], ot_h[:, h, :], m_h[:, at], start=h == 0, stop=False)
                        pe.matmul(out_ps[hf][:, :], ot_h[:, h, :], m_l[:, at], start=False, stop=False)
                        last = pe.matmul(out_ps[hf][:, :], ot_l[:, h, :], m_h[:, at], start=False,
                                         stop=h == HEADS - 1)
                    last.then_inc(out_done, 1)

            def start():
                for h in range(HEADS):
                    for part in range(3):
                        products(h, h % 2, part, start_banks[(3 * h + part) % 4], 3 * h + part - 3)
                    queries(Round(pe, 0), h, (qp_ps, pt_ps)[h % 2], 1)
                rope(Round(pe, 0), 0)
                turn_rope(0)

            def body(before, now, after, more):
                operands = score_operands(now, 0)
                for j in range(QUAD):
                    s = now.slot + j
                    scores(now, j, operands)
                    if after or j < QUAD - 1:
                        if j < QUAD - 1:
                            rope(now, j + 1)
                        else:
                            rope(after, 0)
                    if before or j:
                        if j:
                            outputs(now, j - 1)
                        else:
                            outputs(before, QUAD - 1)
                    pe.wait_ge(norm_step, s * 2 + 2)
                    if before or j:
                        pe.wait_ge(o_lo, s)
                    for h in range(HEADS):
                        turned = pe.transpose(pt_ps[:, h * P:(h + 1) * P], prob[:, h, :], ident)
                    turned.then_inc(pt_done, 1)
                    if after:
                        queries(after, j)
                    if after or j < QUAD - 1:
                        turn_rope(s + 1)
                    if j < QUAD - 1:
                        operands = score_operands(now, j + 1)
                    pe.wait_ge(pt_lo, s + 1)
                    at = bass.ds(now.tok + j * P, P)
                    pe.matmul(pt_ps[:, :], kc_h[:, at], pt_h[:, :], start=True, stop=False)
                    pe.matmul(pt_ps[:, :], kc_l[:, at], pt_h[:, :], start=False, stop=False)
                    pe.matmul(pt_ps[:, :], kc_h[:, at], pt_l[:, :], start=False, stop=True).then_inc(av_done, 1)
                    if more and j:
                        products(now.t + HEADS, now.parity, j - 1, prod_ps, (now.t + HEADS) * 3 + (j - 1))
                if not after:
                    outputs(now, QUAD - 1)

            rounds(pe, start, body)


def ffn_phase(nc, keep, wb_d, ha_d, lb_d, bias_d, out_d):
    with ExitStack() as ctx:
        def sb(name, shape, dt=F32):
            return ctx.enter_context(nc.sbuf_tensor(name, shape, dt))

        def pb(name):
            return ctx.enter_context(nc.psum_tensor(name, [P, CHUNK], F32))

        def sem(name):
            return ctx.enter_context(nc.semaphore(name))

        stage = sb("stage", [P, KT, D])
        raw_ha, raw_lb = sb("raw_ha", [P, KT * HA]), sb("raw_lb", [P, D])
        wb_h, wb_l = sb("wb_h", [P, KT, D], F16), sb("wb_l", [P, KT, D], F16)
        ha_h, ha_l = sb("ha_h", [P, KT, HA], F16), sb("ha_l", [P, KT, HA], F16)
        lb_h, lb_l = sb("lb_h", [P, D], F16), sb("lb_l", [P, D], F16)
        bias = sb("bias", [P, D])
        hid = sb("hid2", [P, D])
        ht_h = [sb(f"fht_h{i}", [P, D], F16) for i in range(2)]
        ht_l = [sb(f"fht_l{i}", [P, D], F16) for i in range(2)]
        result = [sb(f"result{i}", [P, D]) for i in range(2)]
        bn, st, cf, v = sb("fbn", [P, 2, 6]), sb("fst", [P, 2]), sb("fcf", [P, 2]), sb("fv", [P, 3])
        logits = sb("logits", [P, 2 * NE])
        best = sb("best", [P, NE])
        taken = sb("taken", [P, NE])
        left, mask, ex, wsel, comb = (sb(n, [P, 2 * NE if n == "left" else NE])
                                      for n in ("left", "mask", "ex", "wsel", "comb"))
        nbest, wsum, wrec = sb("nbest", [P, 1]), sb("wsum", [P, 1]), sb("wrec", [P, 1])
        hw = sb("hw", [P, NE, RANK])
        hwt_h, hwt_l = sb("hwt_h", [P, P], F16), sb("hwt_l", [P, P], F16)
        turn_ps = [pb("fturn0"), pb("fturn1")]
        ha_ps, hwt_ps = pb("ha_ps"), pb("hwt_ps")
        out_ps = [[pb(f"fout{i}{j}") for j in range(2)] for i in range(2)]
        (pool_passed, dve_passed, filled, ln_step, coef, hid_done, biased, ht_done, ht_hi, ht_lo, ha_done, route_step, ex_done, hw_done,
         hwt_done, hwt_hi, hwt_lo, out_done, result_done, split_hi, split_lo, small_hi, small_lo) = (
            sem(n) for n in (
                "fpool_passed fdve_passed filled fln_step fcoef fhid_done biased fht_done fht_hi fht_lo ha_done route_step ex_done "
                "hw_done hwt_done hwt_hi hwt_lo fout_done result_done split_hi split_lo small_hi small_lo").split())
        stage_loaded = [sem(f"stage_loaded{k}") for k in range(KT)]
        small_loaded = [sem(f"small_loaded{i}") for i in range(3)]
        stored = [sem(f"stored{i}") for i in range(2)]
        COEF = RSQRT_LINKS + 3
        ROUTE = 12
        EARLY = 2
        resid, ident = keep["resid"], keep["consts"][:, 0:P]
        UN = 1.0 / (LN_S * AW_S)
        block = ctx.enter_context(nc.Block())

        @block.sync
        def _(sp):
            sp.dma_start(raw_ha[:, :], ha_d).then_inc(small_loaded[0], 16)
            for k in range(KT):
                sp.dma_start(stage[:, k, :], wb_d[:, k, :]).then_inc(stage_loaded[k], 16)
                if k == 3:
                    sp.dma_start(bias[:, :], bias_d.partition_broadcast(P)).then_inc(small_loaded[2], 16)
            sp.dma_start(raw_lb[:, :], lb_d).then_inc(small_loaded[1], 16)

            def store(b, p):
                sp.wait_ge(result_done, b * 2 + 2)
                sp.dma_start(out_d[bass.ds(b, 1), :, :].rearrange("a p n -> (a p) n"), result[p][:, :]
                             ).then_inc(stored[p], 16)

            with sp.Fori(0, B - 1, 2) as b:
                store(b, 0)
                store(b + 1, 1)
            for p in range(2):
                sp.wait_ge(stored[p], B // 2 * 16)

        @block.scalar
        def _(act):
            act.wait_ge(small_loaded[0], 16)
            act.activation(ha_h[:, :, :].rearrange("p k n -> p (k n)"), raw_ha[:, :], ACT.Copy, scale=AW_S
                           ).then_inc(small_hi, 1)

            def split_weights(tiles):
                for k in tiles:
                    act.wait_ge(stage_loaded[k], 16)
                    act.activation(wb_h[:, k, :], stage[:, k, :], ACT.Copy, scale=AW_S).then_inc(split_hi, 1)

            def body(i, p, ok):
                if ok(0):
                    act.wait_ge(route_step, i * ROUTE + 3)
                    act.activation(ex[:, :], logits[:, 0:NE], ACT.Exp, bias=nbest[:, 0:1], scale=UN
                                   ).then_inc(ex_done, 1)
                if ok(-1):
                    act.wait_ge(coef, i * COEF + 2 * COEF)
                    if not isinstance(i, int) or i >= 0:
                        act.wait_ge(ht_done, i * 2 + 2)
                    act.activation(hid[:, :], resid[:, bass.ds((i + 1) * D, D)], ACT.Identity,
                                   bias=cf[:, 1:2], scale=cf[:, 0:1]).then_inc(hid_done, 1)
                if ok(0):
                    act.wait_ge(hwt_done, i + 1)
                    if not isinstance(i, int) or i >= 1:
                        act.wait_ge(out_done, i * 2)
                    act.activation(hwt_h[:, :], hwt_ps[:, 0:P], ACT.Copy, scale=HW_S * UN).then_inc(hwt_hi, 1)
                if ok(-1):
                    for hf in range(2):
                        act.wait_ge(ht_done, i * 2 + hf + 3)
                        act.activation(ht_h[1 - p][:, hf * CHUNK:(hf + 1) * CHUNK], turn_ps[hf][:, :],
                                       ACT.Copy, scale=LN_S).then_inc(ht_hi, 1)
                if isinstance(i, int) and i == -1:
                    split_weights(range(EARLY, KT))
                    act.wait_ge(small_loaded[1], 16)
                    act.activation(lb_h[:, :], raw_lb[:, :], ACT.Copy, scale=LB_S).then_inc(small_hi, 1)

            split_weights(range(EARLY))
            pipeline(act, body, -1, [-1, 0], 2)

        @block.gpsimd
        def _(pool):
            def body(i, p, ok):
                later = not isinstance(i, int)
                if ok(0):
                    wait_apart(pool, pool_passed, (ln_step, i * 3 + 3))
                    link = Chain(pool, coef, i, COEF, pool_passed)
                    link(pool.tensor_scalar(v[:, 0:1], st[:, 1:2], LN_EPS, None, ALU.add))
                    newton_rsqrt(pool, link, cf[:, 0:1], v[:, 0:1], v[:, 1:2])
                    link(pool.tensor_scalar(v[:, 2:3], st[:, 0:1], -1.0, None, ALU.mult))
                    link(pool.tensor_tensor(cf[:, 1:2], v[:, 2:3], cf[:, 0:1], ALU.mult))
                    if not later and i == 0:
                        pool.wait_ge(small_loaded[2], 16)
                    pool.wait_ge(hid_done, i + 1)
                    at = bass.ds(i * D, D)
                    pool.tensor_tensor(resid[:, at], resid[:, at], bias[:, :], ALU.add).then_inc(biased, 1)

            pipeline(pool, body, 0, [0], 2)

        @block.vector
        def _(dve):
            def low(out, src, scale, high, done):
                dve.scalar_tensor_tensor(out=out, in0=src, scalar=scale, in1=high, op0=ALU.mult,
                                         op1=ALU.subtract).then_inc(done, 1)

            def split_weights(tiles):
                for k in tiles:
                    dve.wait_ge(split_hi, k + 1)
                    low(wb_l[:, k, :], stage[:, k, :], AW_S, wb_h[:, k, :], split_lo)

            dve.memset(logits[:, NE:], SENTINEL).then_inc(filled, 1)
            dve.memset(taken[:, :], SENTINEL).then_inc(filled, 1)

            def body(i, p, ok):
                later = not isinstance(i, int)
                if ok(-2):
                    if later or i >= -1:
                        dve.wait_ge(coef, (i + 2) * COEF)
                    for hf in range(2):
                        dve.bn_stats(bn[:, hf, :], resid[:, bass.ds((i + 2) * D + hf * CHUNK, CHUNK)]
                                     ).then_inc(ln_step, 1)
                    wait_apart(dve, dve_passed, (ln_step, (i + 2) * 3 + 2))
                    dve.bn_aggr(st[:, :], bn[:, :, :]).then_inc(ln_step, 1)
                if not later and i == -2:
                    dve.wait_ge(small_hi, 1)
                    low(ha_l[:, :, :].rearrange("p k n -> p (k n)"), raw_ha[:, :], AW_S,
                        ha_h[:, :, :].rearrange("p k n -> p (k n)"), small_lo)
                    split_weights(range(EARLY))
                if ok(0):
                    dve.wait_ge(ha_done, i + 1)
                    if later or i >= 1:
                        dve.wait_ge(ex_done, i)
                    link = Chain(dve, route_step, i, ROUTE, dve_passed)
                    link(dve.tensor_copy(logits[:, 0:NE], ha_ps[:, NE * RANK:HA]))
                    link(dve.max(best[:, :], logits[:, 0:NE]))
                    link(dve.tensor_scalar(nbest[:, :], best[:, 0:1], -UN, None, ALU.mult))
                    link(dve.tensor_copy(taken[:, 0:2], best[:, 0:2]))
                    link(dve.match_replace(left[:, :], taken[:, :], logits[:, :], SENTINEL))
                    link(dve.tensor_tensor(mask[:, :], left[:, 0:NE], logits[:, 0:NE], ALU.not_equal))
                    dve.wait_ge(ex_done, i + 1)
                    link(dve.tensor_tensor(wsel[:, :], ex[:, :], mask[:, :], ALU.mult))
                    link(dve.tensor_reduce(wsum[:, :], wsel[:, :], AX.X, ALU.add))
                    link(dve.reciprocal(wrec[:, :], wsum[:, :]))
                    link(dve.tensor_scalar(comb[:, :], wsel[:, :], wrec[:, 0:1], LORA_SCALE, ALU.mult, ALU.mult))
                    if later or i >= 1:
                        dve.wait_ge(hwt_done, i)
                    link(dve.tensor_tensor(hw[:, :, :],
                                           ha_ps[:, 0:NE * RANK].rearrange("p (e r) -> p e r", e=NE),
                                           comb[:, :, None].broadcast_to([P, NE, RANK]), ALU.mult))
                    dve.wait_ge(hwt_hi, i + 1)
                    link(dve.scalar_tensor_tensor(out=hwt_l[:, :], in0=hwt_ps[:, 0:P], scalar=HW_S * UN,
                                                  in1=hwt_h[:, :], op0=ALU.mult, op1=ALU.subtract))
                if ok(-1):
                    for hf in range(2):
                        dve.wait_ge(ht_hi, i * 2 + hf + 3)
                        sl = slice(hf * CHUNK, (hf + 1) * CHUNK)
                        low(ht_l[1 - p][:, sl], turn_ps[hf][:, :], LN_S, ht_h[1 - p][:, sl], ht_lo)
                if not later and i == -1:
                    split_weights(range(EARLY, KT))
                    dve.wait_ge(small_hi, 2)
                    low(lb_l[:, :], raw_lb[:, :], LB_S, lb_h[:, :], small_lo)
                if ok(0):
                    if later or i >= 2:
                        dve.wait_ge(stored[p], later_store(i, p))
                    dve.wait_ge(biased, i + 1)
                    for hf in range(2):
                        dve.wait_ge(out_done, i * 2 + hf + 1)
                        dve.scalar_tensor_tensor(out=result[p][:, hf * CHUNK:(hf + 1) * CHUNK],
                                                 in0=out_ps[p][hf][:, :], scalar=UN,
                                                 in1=resid[:, bass.ds(i * D + hf * CHUNK, CHUNK)],
                                                 op0=ALU.mult, op1=ALU.add).then_inc(result_done, 1)

            def later_store(i, p):
                return (i - p) * 8

            dve.wait_ge(filled, 2)
            pipeline(dve, body, -2, [-2, -1, 0], 2)

        @block.tensor
        def _(pe):
            def body(i, p, ok):
                later = not isinstance(i, int)
                if ok(0):
                    pe.wait_ge(ht_lo, i * 2 + 2)
                    if later or i >= 1:
                        pe.wait_ge(route_step, i * ROUTE - 1)
                    n = 0
                    for k in range(KT):
                        for h, w in ((ht_h, ha_h), (ht_h, ha_l), (ht_l, ha_h)):
                            last = pe.matmul(ha_ps[:, 0:HA], h[p][:, k * P:(k + 1) * P], w[:, k, :],
                                             start=n == 0, stop=n == 3 * KT - 1)
                            n += 1
                    last.then_inc(ha_done, 1)
                    if later or i >= 2:
                        pe.wait_ge(result_done, i * 2 - 2)

                    def base(hf):
                        for k in range(KT):
                            if not later and i == 0 and hf == 0:
                                pe.wait_ge(split_lo, k + 1)
                            for n, (h, w) in enumerate(((ht_h, wb_h), (ht_h, wb_l), (ht_l, wb_h))):
                                pe.matmul(out_ps[p][hf][:, :], h[p][:, k * P:(k + 1) * P],
                                          w[:, k, hf * CHUNK:(hf + 1) * CHUNK],
                                          start=k == 0 and n == 0, stop=False)

                    base(0)
                    if not later and i == 0:
                        base(1)
                    pe.wait_ge(route_step, i * ROUTE + 11)
                    pe.transpose(hwt_ps[:, 0:P], hw[:, :, :].rearrange("p e r -> p (e r)"), ident
                                 ).then_inc(hwt_done, 1)
                    if later or i > 0:
                        base(1)
                if ok(-1):
                    pe.wait_ge(hid_done, i + 2)
                    for hf in range(2):
                        if later or i >= 0:
                            pe.wait_ge(ht_lo, i * 2 + hf + 1)
                        for k in range(4):
                            last = pe.transpose(turn_ps[hf][:, k * P:(k + 1) * P],
                                                hid[:, (4 * hf + k) * P:(4 * hf + k + 1) * P], ident)
                        last.then_inc(ht_done, 1)
                if ok(0):
                    if not later and i == 0:
                        pe.wait_ge(small_lo, 2)
                    pe.wait_ge(route_step, i * ROUTE + 12)
                    for hf in range(2):
                        sl = slice(hf * CHUNK, (hf + 1) * CHUNK)
                        pe.matmul(out_ps[p][hf][:, :], hwt_h[:, :], lb_h[:, sl], start=False, stop=False)
                        pe.matmul(out_ps[p][hf][:, :], hwt_h[:, :], lb_l[:, sl], start=False, stop=False)
                        pe.matmul(out_ps[p][hf][:, :], hwt_l[:, :], lb_h[:, sl], start=False, stop=True
                                  ).then_inc(out_done, 1)

            pe.wait_ge(small_lo, 1)
            pipeline(pe, body, -1, [-1, 0], 2)


def build(nc, x_d, wc_d, pw_d, wqk_d, rows_d, params_d, consts_d, heads_d, wb_d, ha_d, lb_d, bias_d, out_d):
    nc.disable_value_cache = True
    with ExitStack() as whole:
        def make(ctx, shapes):
            return {n: ctx.enter_context(nc.sbuf_tensor(n, list(s), dt)) for n, s, dt in shapes}

        keep = make(whole, [("resid", (P, B * D), F32), ("consts", (P, P + 2 * RD), F32),
                            ("ident_h", (P, P), F16), ("mean_mat", (P, P), F32)])
        with ExitStack() as first_two:
            latents = [("qct", (P, QT, TOK)), ("kct", (P, TOK)), ("kc", (P, TOK)), ("kr", (P, TOK))]
            keep.update(make(first_two, [(f"{n}_{part}", s, F16) for n, s in latents for part in "hl"]))
            keep.update(make(first_two, [(f"wide{i}", (P, XW), F32) for i in range(2)]))
            raw_loaded = [first_two.enter_context(nc.semaphore(f"raw_loaded{i}")) for i in range(2)]
            with ExitStack() as first:
                keep.update(make(first, [
                    ("params", (P, 10), F32), ("gains", (P, QR + KVR), F32),
                    ("wc_h", (P, PAIRS * CH), F16), ("wc_l", (P, PAIRS * CH), F16),
                    ("pw_h", (P, CH), F16), ("pw_l", (P, CH), F16),
                    ("wqk_h", (P, KT * (QR + KVR + RD)), F16), ("wqk_l", (P, KT * (QR + KVR + RD)), F16)]))
                token_phase(nc, keep, raw_loaded, x_d, wc_d, wqk_d, pw_d, rows_d, params_d, consts_d, heads_d)
            nc.disable_value_cache = False
            attention_phase(nc, keep, raw_loaded, heads_d)
            nc.disable_value_cache = True
        ffn_phase(nc, keep, wb_d, ha_d, lb_d, bias_d, out_d)


def rotary_tables(np):
    inv_freq = 1.0 / np.float32(10000.0) ** (np.arange(0, RD, 2, dtype=np.float32) / np.float32(RD))
    angles = np.outer(np.arange(CH, dtype=np.float32), inv_freq).astype(np.float32)
    c, s = np.cos(angles), np.sin(angles)
    return np.concatenate([c, c, -s, s], axis=1).astype(np.float32)


def kernel(**inputs):
    import numpy as np
    import concourse.bacc as bacc
    from concourse.bass_utils import run_bass_kernel_spmd

    a = {n.removeprefix("L0_"): np.asarray(v) for n, v in inputs.items()}
    taps = np.concatenate([a["tok_conv_in_w"], np.zeros((CH, CI, 1), np.float32)], axis=2)
    wc = taps.reshape(CH, CI, PAIRS, 2).transpose(3, 1, 2, 0).reshape(P, PAIRS * CH)
    wqk = np.concatenate([a["attn_w_qa"], a["attn_w_kva"]], axis=1)
    wqk = wqk.reshape(KT, P, QR + KVR + RD).transpose(1, 0, 2).reshape(P, -1)
    params = np.concatenate([a["tok_dw_w"][:, 0, :], np.stack([a[f"tok_{n}"] for n in (
        "dw_b", "gn1_w", "gn1_b", "gn2_w", "gn2_b")], axis=1)], axis=1)
    wqb = a["attn_w_qb"].reshape(QR, NH, QK)
    wkv = a["attn_w_kvb"].reshape(KVR, NH, 2, P)
    heads = np.concatenate([
        wqb[:, :, 0:P].transpose(1, 2, 0),
        wkv[:, :, 0].transpose(1, 2, 0), wkv[:, :, 1].transpose(1, 2, 0),
        a["attn_w_o"].reshape(NH, P, D),
        wqb[:, :, P:].reshape(QT, P, NH, RD).transpose(2, 1, 0, 3).reshape(NH, P, QT * RD)], axis=2)
    ha = np.concatenate([a["ffn_A"].reshape(NE * RANK, D), a["ffn_W_router"]], axis=0)
    arrays = {
        "x": a["x"], "wc": wc, "pw": a["tok_pw_w"][:, :, 0].T, "wqk": wqk,
        "rows": np.concatenate([a["attn_g_qa"], a["attn_g_kva"]]), "params": params,
        "consts": np.concatenate([np.eye(P, dtype=np.float32), rotary_tables(np)], axis=1),
        "heads": heads, "wb": a["ffn_W_base"].T.reshape(KT, P, D).transpose(1, 0, 2),
        "ha": ha.T.reshape(KT, P, HA).transpose(1, 0, 2).reshape(P, KT * HA),
        "lb": a["ffn_B"].transpose(0, 2, 1).reshape(NE * RANK, D), "bias": a["ffn_b_base"],
    }
    arrays = {f"{n}_in": np.ascontiguousarray(v) for n, v in arrays.items()}
    nc = bacc.Bacc("TRN2", target_bir_lowering=False, num_devices=1)
    args = [nc.dram_tensor(n, v.shape, mybir.dt.from_np(v.dtype), kind="ExternalInput").ap()
            for n, v in arrays.items()]
    args.append(nc.dram_tensor("tower_out", (B, CH, D), F32, kind="ExternalOutput").ap())
    build(nc, *args)
    ran = run_bass_kernel_spmd(nc, [arrays], core_ids=[0])
    return ran.results[0]["tower_out"]
```
